# Optimizing a Trainium2 kernel written in Bass

```python
import numpy as np
import jax
import jax.numpy as jnp

def _softmax(x, axis=-1):
    return jax.nn.softmax(x, axis=axis)

def _gelu(x):
    return jax.nn.gelu(x, approximate=True)

def _silu(x):
    return jax.nn.silu(x)

def _sigmoid(x):
    return jax.nn.sigmoid(x)

def _layernorm(x, axis=-1, eps=1e-05):
    m = jnp.mean(x, axis=axis, keepdims=True)
    v = jnp.var(x, axis=axis, keepdims=True)
    return (x - m) / jnp.sqrt(v + eps)

def _scatter_add(tgt, idx, src, axis=0):
    return tgt.at[idx].add(src)

def _segment_sum(src, seg, n):
    return jax.ops.segment_sum(src, seg, n)
kernel_name = 'mk_adaln_d1_jaxref_r8_9ac680'

def setup_inputs(seed: int=0):
    np.random.seed(seed)
    _w = jnp.asarray

    def _L0_attn_setup():
        import jax, jax.numpy as jnp
        import numpy as np
        B, S, D = (1, 512, 128)
        H, W = (16, 64)
        HD = D // H
        key = jax.random.key(seed)
        k1, k2, k3 = jax.random.split(key, 3)
        x = jax.random.normal(k1, (B, S, D), dtype=jnp.float32)
        w_qkv = jax.random.normal(k2, (D, 3 * D), dtype=jnp.float32) * 0.02
        w_out = jax.random.normal(k3, (D, D), dtype=jnp.float32) * 0.02
        return {'x': x, 'w_qkv': w_qkv, 'w_out': w_out}
    _L0_attn_in = _L0_attn_setup()

    def _L0_ffn_setup():
        import jax, jax.numpy as jnp
        import numpy as np
        DIM = 128
        HID = 352
        E = 8
        TOPK = 2
        B, S = (4, 128)
        key = jax.random.key(seed)
        k_x, k_g, k1, k2, k3 = jax.random.split(key, 5)
        scale_d = 1.0 / np.sqrt(DIM)
        scale_h = 1.0 / np.sqrt(HID)
        return {'x': jax.random.normal(k_x, (B, S, DIM), dtype=jnp.float32), 'Wg': jax.random.normal(k_g, (E, DIM), dtype=jnp.float32) * scale_d, 'W1': jax.random.normal(k1, (E, HID, DIM), dtype=jnp.float32) * scale_d, 'W3': jax.random.normal(k3, (E, HID, DIM), dtype=jnp.float32) * scale_d, 'W2': jax.random.normal(k2, (E, DIM, HID), dtype=jnp.float32) * scale_h}
    _L0_ffn_in = _L0_ffn_setup()
    _L0_c = _w((lambda *s: np.random.randn(*s).astype(np.float32) * 0.05)(8, 128))
    _L0_wmod = _w((lambda *s: np.random.randn(*s).astype(np.float32) * 0.05)(128, 6 * 128) * 128 ** (-0.5))
    _d = {'L0_attn_x': _L0_attn_in['x'], 'L0_attn_w_qkv': _L0_attn_in['w_qkv'], 'L0_attn_w_out': _L0_attn_in['w_out'], 'L0_ffn_Wg': _L0_ffn_in['Wg'], 'L0_ffn_W1': _L0_ffn_in['W1'], 'L0_ffn_W3': _L0_ffn_in['W3'], 'L0_ffn_W2': _L0_ffn_in['W2'], 'L0_c': _L0_c, 'L0_wmod': _L0_wmod}
    _x0 = _d['L0_attn_x']
    _d['L0_attn_x'] = jax.random.normal(jax.random.fold_in(jax.random.key(seed), 1), (8, 256, 128), dtype=_x0.dtype)
    del _x0
    return _d

def reference(L0_attn_x, L0_attn_w_qkv, L0_attn_w_out, L0_ffn_Wg, L0_ffn_W1, L0_ffn_W3, L0_ffn_W2, L0_c, L0_wmod):

    def _L0_attn_ref(x, w_qkv, w_out):
        import jax, jax.numpy as jnp
        import numpy as np
        B, S, D = (1, 512, 128)
        H, W = (16, 64)
        HD = D // H
        b, s, d = x.shape
        qkv = x @ w_qkv
        q, k, v = jnp.split(qkv, 3, axis=-1)
        to_heads = lambda t: t.reshape(b, s, H, HD).transpose(0, 2, 1, 3)
        q, k, v = map(to_heads, (q, k, v))
        C = s // W
        qc = q.reshape(b, H, C, W, HD)
        kc = k.reshape(b, H, C, W, HD)
        vc = v.reshape(b, H, C, W, HD)
        zero = jnp.zeros_like(kc[:, :, :1])
        k_prev = jnp.concatenate([zero, kc[:, :, :-1]], axis=2)
        v_prev = jnp.concatenate([jnp.zeros_like(vc[:, :, :1]), vc[:, :, :-1]], axis=2)
        kcat = jnp.concatenate([k_prev, kc], axis=3)
        vcat = jnp.concatenate([v_prev, vc], axis=3)
        scores = jnp.einsum('bhcqd,bhckd->bhcqk', qc, kcat) / HD ** 0.5
        wq = jnp.arange(W)
        jk = jnp.arange(2 * W)
        ci = jnp.arange(C)
        causal = wq[:, None] + W >= jk[None, :]
        valid = ci[:, None, None] * W + jk[None, None, :] - W >= 0
        mask = causal[None] & valid
        scores = jnp.where(mask[None, None], scores, -jnp.inf)
        attn = jax.nn.softmax(scores, axis=-1)
        out = jnp.einsum('bhcqk,bhckd->bhcqd', attn, vcat)
        out = out.reshape(b, H, s, HD).transpose(0, 2, 1, 3).reshape(b, s, d)
        return out @ w_out

    def _L0_ffn_ref(x, Wg, W1, W3, W2):
        import jax, jax.numpy as jnp
        import numpy as np
        DIM = 128
        HID = 352
        E = 8
        TOPK = 2
        B, S = (4, 128)
        Bsz, Ssz, D = x.shape
        xt = x.reshape(Bsz * Ssz, D)
        scores = xt @ Wg.T
        top_vals, top_idx = jax.lax.top_k(scores, TOPK)
        weights = jax.nn.softmax(top_vals, axis=-1)
        h1 = jnp.einsum('td,ehd->teh', xt, W1)
        h3 = jnp.einsum('td,ehd->teh', xt, W3)
        expert_out = jnp.einsum('teh,edh->ted', jax.nn.silu(h1) * h3, W2)
        idx = top_idx[:, :, None]
        sel = jnp.take_along_axis(expert_out, idx, axis=1)
        out = jnp.sum(sel * weights[:, :, None], axis=1)
        return out.reshape(Bsz, Ssz, D)
    x = L0_attn_x
    mod = (_silu(L0_c) @ L0_wmod).reshape(L0_c.shape[0], 6, 1, -1)
    sa, ca, ga, sb, cb, gb = (mod[:, 0], mod[:, 1], mod[:, 2], mod[:, 3], mod[:, 4], mod[:, 5])
    ga = (2 * (ga >= 0) - 1) * jnp.maximum(jnp.abs(ga), 0.25)
    gb = (2 * (gb >= 0) - 1) * jnp.maximum(jnp.abs(gb), 0.25)
    h = _layernorm(x, axis=-1) * (1 + ca) + sa
    x = x + ga * _L0_attn_ref(h, L0_attn_w_qkv, L0_attn_w_out)
    h = _layernorm(x, axis=-1) * (1 + cb) + sb
    x = x + gb * _L0_ffn_ref(h, L0_ffn_Wg, L0_ffn_W1, L0_ffn_W3, L0_ffn_W2)
    return x

_drawn_inputs = setup_inputs


def setup_inputs(seed=0):
    import zlib

    import numpy as np

    out = dict(_drawn_inputs(seed))
    spreads = {}
    factors = {'L0_attn_w_qkv': 8.0, 'L0_attn_w_out': 8.0}
    for name, (base, spread) in spreads.items():
        noise = np.random.default_rng([zlib.crc32(name.encode()), seed]).standard_normal(out[name].shape)
        drawn = base * np.exp(spread * noise) if base else spread * noise
        out[name] = jnp.asarray(drawn.astype(out[name].dtype))
    for name, factor in factors.items():
        out[name] = (out[name] * factor).astype(out[name].dtype)
    return out
```

```python
from contextlib import ExitStack

import concourse.bass as bass
from concourse import mybir

F32 = mybir.dt.float32
BF16 = mybir.dt.bfloat16
I32 = mybir.dt.int32
U32 = mybir.dt.uint32
ALU = mybir.AluOpType
ACT = mybir.ActivationFunctionType
AX_X = mybir.AxisListType.X

P = 128
B, S, D = 8, 256, 128
H, W = 16, 64
HD = D // H
E, TOPK, HID = 8, 2, 352
EPS = 1e-5
NT = B * S // P
TOKENS = B * S
REGION = TOKENS + P
N_ROWS = E * REGION + P
N_SLOTS = -(-(TOPK * TOKENS // P + E - 1) // 4) * 4
PAY = D + 1
HIDP = 384
KT = HIDP // P
LANE = 40
WIN = W + S
OUT_OF_RANGE = 1.0e6
MASKED = -1.0e30

CF = {}
CB = {}


def _columns(table, names):
    at = 0
    for name, n in names:
        table[name] = (at, at + n)
        at += n
    return at


N_CF = _columns(CF, [("ident", P), ("headmask", H), ("iota8", E), ("base8", E), ("tokid", 2 * NT),
                     ("steps", E * NT), ("tri8", E * E), ("slot", N_SLOTS * E), ("padrow", PAY), ("half", 2)])
N_CB = _columns(CB, [("ident", P), ("before", P), ("ones", P), ("mask0", 4 * P), ("mask1", 4 * W)])


def build(nc, x, c_t, wqkv, wout, wmod, wg_t, w13, w2, cf, cb, out):
    routed = nc.dram_tensor("routed", [N_ROWS, PAY], F32, kind="Internal").ap()
    ranked = nc.dram_tensor("ranked", [TOPK * TOKENS, D], F32, kind="Internal").ap()
    mod_rows = nc.dram_tensor("mod_rows", [B, 4 * D], F32, kind="Internal").ap()

    with ExitStack() as ctx:
        def sb(name, shape, dt=F32):
            return ctx.enter_context(nc.sbuf_tensor(name, shape, dt))

        def sem(name):
            return ctx.enter_context(nc.semaphore(name))

        bank = [ctx.enter_context(nc.psum_tensor(f"bank{i}", [P, 512], F32)) for i in range(8)]
        S_BANK = bank[0:3]
        PT_BANK = bank[3]
        O_BANK = bank[4]
        M = bank[5:8]
        XT_BANK, H1_BANK, H3_BANK = bank[0], bank[1:3], bank[3:5]
        GT_BANK, Y_BANK = (bank[5], bank[7]), bank[6]

        cf_sb = sb("cf_sb", [P, N_CF])
        cb_sb = sb("cb_sb", [P, N_CB], BF16)
        ct_sb = sb("ct_sb", [P, B])
        wqkv_sb = sb("wqkv_sb", [P, 3 * D])
        wout_sb = sb("wout_sb", [P, D])
        wmod_sb = sb("wmod_sb", [P, 6 * D])
        wg_sb = sb("wg_sb", [P, E])
        w13_sb = sb("w13_sb", [P, E * 2 * HID])
        w2_sb = sb("w2_sb", [P, E * KT * D])
        silu_c = sb("silu_c", [P, B])
        mod_t = sb("mod_t", [P, 2 * B])
        mod_s = sb("mod_s", [B, 4 * D])
        mod_a = sb("mod_a", [B, 2, D])
        mod_b = sb("mod_b", [B, 2, D])
        mod_bc = sb("mod_bc", [P, B * 4 * D])
        x_all = sb("x_all", [P, NT, D])
        stats = sb("stats", [P, 2, 6])
        mv = sb("mv", [P, 2, 2])
        veps = sb("veps", [P, 2])
        rstd = sb("rstd", [P, 2])
        normed = sb("normed", [P, 2, D])
        h_t = sb("h_t", [P, WIN])
        q_t = [sb(f"q_t{i}", [P, S]) for i in range(2)]
        k_sb = sb("k_sb", [P, S])
        k_diag = sb("k_diag", [P, 4, 4, WIN])
        v_lane = [sb(f"v_lane{i}", [P, 4 * H * LANE + LANE]) for i in range(2)]
        negmax = sb("negmax", [P, 4, 4])
        probs = [sb(f"probs{i}", [P, 4, P]) for i in range(2)]
        probs_t = [sb(f"probs_t{i}", [P, 4, P]) for i in range(2)]
        den = [sb(f"den{i}", [P, H]) for i in range(2)]
        rden = sb("rden", [P, H])
        rden_w = [sb(f"rden_w{i}", [P, H, HD]) for i in range(2)]
        o_sb = sb("o_sb", [P, P])
        o_n = sb("o_n", [P, P])
        yg = sb("yg", [P, D])
        stats2 = sb("stats2", [P, 6])
        mv2 = sb("mv2", [P, 2])
        veps2 = sb("veps2", [P, 1])
        rstd2 = sb("rstd2", [P, 1])
        n2 = sb("n2", [P, D])
        n2c = sb("n2c", [P, D])
        pay = [sb(f"pay{i}", [P, TOPK, PAY]) for i in range(2)]
        h2_t = sb("h2_t", [P, P])
        sc8 = sb("sc8", [P, E])
        top8 = sb("top8", [P, 8])
        ix8 = sb("ix8", [P, 8], U32)
        ixf = sb("ixf", [P, 2])
        top_v = sb("top_v", [P, NT * 2])
        hot = [sb(f"hot{i}", [P, 2, E]) for i in range(2)]
        hot_b = [sb(f"hot_b{i}", [P, E], BF16) for i in range(2)]
        hot_sum = sb("hot_sum", [P, E], BF16)
        pos = sb("pos", [P, E])
        junk = sb("junk", [P, 2, E])
        row_f = sb("row_f", [P, 2])
        row_u = [sb(f"row_u{i}", [P, 2], U32) for i in range(2)]
        n_e = sb("n_e", [1, E])
        cmp_e = sb("cmp_e", [1, E, NT])
        tiles_e = sb("tiles_e", [1, E])
        cum_m = sb("cum_m", [1, E, E])
        cum_e = sb("cum_e", [1, E])
        ge = sb("ge", [1, N_SLOTS, E])
        ge_t = sb("ge_t", [1, N_SLOTS, E])
        slot_e = sb("slot_e", [1, N_SLOTS])
        slot_b = sb("slot_b", [1, N_SLOTS])
        slot_r = sb("slot_r", [1, N_SLOTS])
        slot_w = sb("slot_w", [1, N_SLOTS])
        table = sb("table", [1, 3 * N_SLOTS + E], I32)
        xt_in = [sb(f"xt_in{i}", [P, PAY]) for i in range(4)]
        ix_u = [sb(f"ix_u{i}", [P, 1], U32) for i in range(4)]
        x_t = [sb(f"x_t{i}", [P, P]) for i in range(2)]
        act1 = [sb(f"act1_{i}", [P, HID]) for i in range(2)]
        gated = [sb(f"gated{i}", [P, HIDP]) for i in range(2)]
        gated_t = [sb(f"gated_t{i}", [P, HIDP]) for i in range(2)]
        y_sb = [sb(f"y_sb{i}", [P, D]) for i in range(4)]
        fin_a = sb("fin_a", [P, NT, D])
        fin_b = sb("fin_b", [P, NT, D])
        ex = sb("ex", [P, NT])
        exd = sb("exd", [P, NT])
        w_hi = sb("w_hi", [P, NT])
        w_lo = sb("w_lo", [P, NT])

        def cf_(name, rows=P):
            a, z = CF[name]
            return cf_sb[0:rows, a:z]

        def cb_(name):
            a, z = CB[name]
            return cb_sb[:, a:z]

        ident, ident_b, headmask = cf_("ident"), cb_("ident"), cf_("headmask")

        def mod(b, which):
            return mod_bc[:, bass.ds((b * 4 + which) * D, D)]

        def x_tile(t):
            return x_all[:, bass.ds(t, 1), :].rearrange("p a d -> p (a d)")

        ld_c = sem("ld_c")
        ld_x0 = sem("ld_x0")
        ld_w = sem("ld_w")
        ld_x = sem("ld_x")
        ld_e = sem("ld_e")
        mod_out = sem("mod_out")
        mod_in = sem("mod_in")
        silu_done = sem("silu_done")
        mod_mm = sem("mod_mm")
        mod_done = sem("mod_done")
        zeroed = sem("zeroed")
        scores_done = sem("scores_done")
        negmax_done = sem("negmax_done")
        probs_done = sem("probs_done")
        pt_done = sem("pt_done")
        pt_copied = sem("pt_copied")
        pv_done = sem("pv_done")
        var_ready = sem("var_ready")
        rstd_ready = sem("rstd_ready")
        normed_ready = sem("normed_ready")
        nt_done = sem("nt_done")
        ht_ready = sem("ht_ready")
        qk_done = sem("qk_done")
        qk_copied = sem("qk_copied")
        kdiag_act = sem("kdiag_act")
        kdiag_pool = sem("kdiag_pool")
        v_done = sem("v_done")
        v_copied = sem("v_copied")
        o_copied = sem("o_copied")
        rden_ready = sem("rden_ready")
        rt_done = sem("rt_done")
        on_ready = sem("on_ready")
        y_done = sem("y_done")
        var2_ready = sem("var2_ready")
        rstd2_ready = sem("rstd2_ready")
        h2_ready = sem("h2_ready")
        pay_ready = sem("pay_ready")
        h2t_done = sem("h2t_done")
        h2t_copied = sem("h2t_copied")
        gate_done = sem("gate_done")
        hot_ready = sem("hot_ready")
        prefix_done = sem("prefix_done")
        rows_ready = sem("rows_ready")
        scattered = [sem(f"scattered{i}") for i in range(2)]
        dve_link = sem("dve_link")
        pool_link = sem("pool_link")
        count_done = sem("count_done")
        table_ready = sem("table_ready")
        padded = sem("padded")
        xt_loaded = [sem(f"xt_loaded{i}") for i in range(4)]
        xt_done = sem("xt_done")
        xt_copied = sem("xt_copied")
        ix_ready = sem("ix_ready")
        h1_done = sem("h1_done")
        h3_done = sem("h3_done")
        act1_ready = sem("act1_ready")
        gated_ready = sem("gated_ready")
        gt_done = sem("gt_done")
        gt_copied = sem("gt_copied")
        ye_done = sem("ye_done")
        ye_copied = sem("ye_copied")
        y_out = [sem(f"y_out{i}") for i in range(4)]
        fin_in = [sem(f"fin_in{i}") for i in range(4)]
        ex_ready = sem("ex_ready")
        fin_done = sem("fin_done")
        fin_out = sem("fin_out")

        SCORE_BANK = (0, 1, 2, 0, 1, 2, 0, 1)
        SCORE_AGO = (2, 2, 5, 3, 3, 3, 3, 3)

        block = ctx.enter_context(nc.Block())

        def over_batches(eng, body):
            body(0, 0, True, False)
            with eng.Fori(0, B // 2 - 1) as k:
                body(k * 2 + 1, 1, False, False)
                body(k * 2 + 2, 0, False, False)
            body(B - 1, 1, False, True)

        def counter(eng, name):
            r = eng.alloc_register(f"{name}_count")
            eng.reg_mov(r, 0)
            return r

        @block.sync
        def _(sp):
            xv = x.rearrange("b (a p) d -> p (b a) d", p=P)
            sp.dma_start(ct_sb[:, :], c_t).then_inc(ld_c, 16)
            sp.dma_start(wmod_sb[:, :], wmod).then_inc(ld_c, 16)
            sp.dma_start(x_all[:, 0:2, :], xv[:, 0:2, :]).then_inc(ld_x0, 16)
            sp.dma_start(cf_sb[:, :], cf).then_inc(ld_x0, 16)
            sp.dma_start(wqkv_sb[:, :], wqkv).then_inc(ld_w, 16)
            sp.dma_start(cb_sb[:, :], cb).then_inc(ld_w, 16)
            sp.dma_start(wout_sb[:, :], wout).then_inc(ld_w, 16)
            sp.dma_start(wg_sb[:, :], wg_t).then_inc(ld_w, 16)
            sp.dma_start(x_all[:, 2:NT, :], xv[:, 2:NT, :]).then_inc(ld_x, 16)
            sp.wait_ge(mod_done, 2)
            sp.dma_start(mod_rows, mod_s[:, :]).then_inc(mod_out, 16)
            sp.wait_ge(mod_out, 16)
            sp.dma_start(mod_bc[:, :], mod_rows.rearrange("b n -> (b n)").partition_broadcast(P)).then_inc(mod_in, 16)
            sp.dma_start(w13_sb[:, :], w13).then_inc(ld_e, 16)
            sp.dma_start(w2_sb[:, :], w2).then_inc(ld_e, 16)

            sp.wait_ge(table_ready, 1)
            for e in range(E):
                row = sp.value_load(table[0:1, 3 * N_SLOTS + e:3 * N_SLOTS + e + 1],
                                    min_val=0, max_val=N_ROWS - P)
                sp.dma_start(routed[bass.ds(row, P), :], cf_("padrow")).then_inc(padded, 16)
            sp.wait_ge(padded, 16 * E)
            for r in scattered:
                sp.wait_ge(r, 16 * NT + 16)

            def load(s, r):
                if not (isinstance(s, int) and s < 4):
                    sp.wait_ge(xt_done, s - 3)
                    sp.wait_ge(ix_ready, s - 3)
                row = sp.value_load(table[0:1, bass.ds(s, 1)], min_val=0, max_val=N_ROWS - P)
                sp.dma_start(xt_in[r][:, :], routed[bass.ds(row, P), :]).then_inc(xt_loaded[r], 16)

            for s in range(4):
                load(s, s)
            with sp.Fori(1, N_SLOTS // 4) as k:
                for r in range(4):
                    load(k * 4 + r, r)

            for r in range(4):
                sp.wait_ge(y_out[r], 16 * (N_SLOTS // 4))
            rv = ranked.rearrange("(k t p) d -> k p t d", k=2, p=P)
            n = NT // 4
            for i in range(4):
                sp.dma_start(fin_a[:, n * i:n * i + n, :], rv[0, :, n * i:n * i + n, :]).then_inc(fin_in[i], 16)
                sp.dma_start(fin_b[:, n * i:n * i + n, :], rv[1, :, n * i:n * i + n, :]).then_inc(fin_in[i], 16)
            ov = out.rearrange("b (a p) d -> p (b a) d", p=P)
            for i in range(4):
                sp.wait_ge(fin_done, i + 1)
                sp.dma_start(ov[:, n * i:n * i + n, :], fin_a[:, n * i:n * i + n, :]).then_inc(fin_out, 16)
            sp.wait_ge(fin_out, 64)

        STAGES = (("x", 2), ("h", 1), ("t", 0), ("y", -1))

        def over_slots(eng, step):
            def at_end(s):
                step(s, s % 4, [c for c, d in STAGES if 0 <= s + d < N_SLOTS])
            for s in range(-2, 5):
                at_end(s)
            with eng.Fori(1, N_SLOTS // 4 - 1) as k:
                for r in range(4):
                    step(k * 4 + (1 + r), (1 + r) % 4, [c for c, _ in STAGES])
            for s in range(N_SLOTS - 3, N_SLOTS + 1):
                at_end(s)

        def after(s, n):
            return not isinstance(s, int) or s >= n

        @block.tensor
        def _(pe):
            mm = pe.matmul
            pe.wait_ge(ld_c, 32)
            pe.wait_ge(silu_done, 1)
            mm(M[0][0:B, :], silu_c[:, :], wmod_sb[:, 0:512], start=True, stop=True)
            mm(M[1][0:B, 0:256], silu_c[:, :], wmod_sb[:, 512:768], start=True, stop=True)
            mm(M[2][:, 0:B], wmod_sb[:, D:2 * D], silu_c[:, :], start=True, stop=True)
            mm(M[2][:, B:2 * B], wmod_sb[:, 0:D], silu_c[:, :], start=True, stop=True).then_inc(mod_mm, 1)

            def norm_t(b):
                pe.wait_ge(normed_ready, b + 1)
                pe.transpose(M[2][:, 0:P], normed[:, 0, :], ident)
                pe.transpose(M[2][:, P:2 * P], normed[:, 1, :], ident).then_inc(nt_done, 1)

            def project_qk(b):
                pe.wait_ge(ht_ready, b + 1)
                mm(M[2][:, 0:S], wqkv_sb[:, 0:D], h_t[:, W:WIN], start=True, stop=True)
                mm(M[2][:, S:2 * S], wqkv_sb[:, D:2 * D], h_t[:, W:WIN], start=True, stop=True).then_inc(qk_done, 1)

            def project_v():
                for c in range(4):
                    last = mm(M[0][:, c * P:(c + 1) * P], h_t[:, c * W:c * W + 2 * W], wqkv_sb[:, 2 * D:3 * D],
                              start=True, stop=True)
                last.then_inc(v_done, 1)

            def scores(b, par, i):
                g = b * 8 + i
                pair, quad = i // 4, i % 4
                if i == 0:
                    pe.wait_ge(qk_copied, b + 1)
                    pe.wait_ge(kdiag_act, b + 1)
                if 0 < i < 4:
                    pe.wait_ge(kdiag_pool, b * 3 + quad)
                if after(g, 3):
                    pe.wait_ge(probs_done, g + 1 - SCORE_AGO[i])
                s_bank = S_BANK[SCORE_BANK[i]]
                sv = s_bank[:, :].rearrange("p (h k) -> p h k", h=4)
                if pair == 0:
                    mm(s_bank[:, :], ident_b, cb_("mask0"), start=True, stop=False, skip_group_check=True)
                else:
                    mm(sv[:, :, W:2 * W], ident_b, cb_("mask1").rearrange("p (h k) -> p h k", h=4),
                       start=True, stop=False, skip_group_check=True)
                for a in range(2):
                    c = 2 * pair + a
                    last = mm(sv[a * W:(a + 1) * W, :, :], q_t[par][:, c * W:(c + 1) * W],
                              k_diag[:, quad, :, c * W:c * W + 2 * W], start=False, stop=True,
                              skip_group_check=True)
                last.then_inc(scores_done, 1)

            def probs_transpose(g, i):
                pe.wait_ge(probs_done, g + 1)
                if after(g, 1):
                    pe.wait_ge(pt_copied, g)
                for j in range(4):
                    last = pe.transpose(PT_BANK[:, j * P:(j + 1) * P], probs[i % 2][:, j, :], ident)
                last.then_inc(pt_done, 1)

            def pv(b, par, i):
                pair, quad = i // 4, i % 4
                pe.wait_ge(pt_copied, b * 8 + i + 1)
                if i == 0:
                    pe.wait_ge(v_copied, b + 1)
                if quad == 0 and after(b * 8 + i, 1):
                    pe.wait_ge(o_copied, b * 2 + pair)
                for a in range(2):
                    c = 2 * pair + a
                    for j in range(4):
                        at = (c * H + 4 * j + quad) * LANE + 3 * HD - quad * HD
                        last = mm(O_BANK[32 * j:32 * j + 32, a * W:(a + 1) * W], v_lane[par][:, at:at + 32],
                                  probs_t[i % 2][:, j, a * W:(a + 1) * W], start=(quad == 0 and a == 0),
                                  stop=(quad == 3), skip_group_check=True)
                last.then_inc(pv_done, 1)

            def rden_t(t, p, m):
                pe.wait_ge(rden_ready, t + 1)
                pe.transpose(M[m][:, 0:P], rden_w[p][:, :, :].rearrange("p h d -> p (h d)"),
                             ident).then_inc(rt_done, 1)

            def out_project(t, m):
                pe.wait_ge(on_ready, t + 1)
                mm(M[m][:, 0:D], o_n[:, :], wout_sb[:, :], start=True, stop=True).then_inc(y_done, 1)

            def h2_transpose(t, p, m):
                pe.wait_ge(h2_ready, t + 1)
                pe.transpose(M[m][:, 0:P], pay[p][:, 0, 0:D], ident).then_inc(h2t_done, 1)

            def gate(t, m, at):
                pe.wait_ge(h2t_copied, t + 1)
                mm(M[m][:, at:at + E], h2_t[:, :], wg_sb[:, :], start=True, stop=True,
                   skip_group_check=True).then_inc(gate_done, 1)

            def prefix(t, p, m, at):
                pe.wait_ge(hot_ready, t + 1)
                mm(M[m][:, at:at + E], cb_("before"), hot_b[p][:, :], start=True, stop=False,
                   skip_group_check=True)
                mm(M[m][:, at:at + E], cb_("ones"), hot_sum[:, :], start=False, stop=True,
                   skip_group_check=True).then_inc(prefix_done, 1)

            def spare(b, par, i, first, last):
                t0 = b * 2
                p0, p1 = t0 - 2, t0 - 1
                if i == 0 and not first:
                    pe.wait_ge(v_copied, b + 1)
                    rden_t(p1, 1, 0)
                    h2_transpose(p0, 0, 1)
                if i == 1 and not last:
                    pe.wait_ge(kdiag_act, b + 1)
                    norm_t(b + 1)
                if i == 2 and not first:
                    out_project(p1, 0)
                    gate(p0, 0, D)
                if i == 3 and not last:
                    project_qk(b + 1)
                if i == 4:
                    if not first:
                        pe.wait_ge(h2t_copied, b * 2 - 1)
                    rden_t(t0, 0, 1)
                    if not first:
                        prefix(p0, 0, 1, P)
                    if not last:
                        if first:
                            pe.wait_ge(v_copied, 1)
                        else:
                            pe.wait_ge(h2_ready, b * 2)
                            pe.wait_ge(hot_ready, b * 2 - 1)
                        project_v()
                if i == 5 and not first:
                    if not last:
                        pe.wait_ge(kdiag_act, b + 2)
                    h2_transpose(p1, 1, 2)
                if i == 6:
                    if not first:
                        pe.wait_ge(rows_ready, b * 2 - 1)
                    out_project(t0, 1)
                    if not first:
                        gate(p1, 1, D)
                if i == 7 and not first:
                    if not last:
                        pe.wait_ge(v_copied, b + 2)
                    prefix(p1, 1, 0, 0)

            def batch(b, par, first, last):
                for i in range(8):
                    if i + 2 < 8:
                        scores(b, par, i + 2)
                    elif not last:
                        scores(b + 1, 1 - par, i + 2 - 8)
                    probs_transpose(b * 8 + i, i)
                    if i > 0:
                        pv(b, par, i - 1)
                    elif not first:
                        pv(b - 1, 1 - par, 7)
                    spare(b, par, i, first, last)

            pe.wait_ge(mod_done, 2)
            pe.wait_ge(ld_x0, 32)
            pe.wait_ge(ld_w, 64)
            norm_t(0)
            project_qk(0)
            project_v()
            scores(0, 0, 0)
            scores(0, 0, 1)
            over_batches(pe, batch)
            t = NT - 1
            pv(B - 1, 1, 7)
            pe.wait_ge(rows_ready, t - 1)
            rden_t(t, 1, 0)
            pe.wait_ge(hot_ready, t - 1)
            h2_transpose(t - 1, 0, 1)
            gate(t - 1, 2, 0)
            out_project(t, 0)
            prefix(t - 1, 0, 2, 0)
            h2_transpose(t, 1, 1)
            pe.wait_ge(rows_ready, t)
            gate(t, 2, 0)
            prefix(t, 1, 2, 0)
            pe.wait_ge(rows_ready, NT)
            mm(M[1][:, 0:E], cb_("ones"), hot_sum[:, :], start=True, stop=True).then_inc(count_done, 1)

            pe.wait_ge(ld_e, 32)
            pe.wait_ge(table_ready, 1)

            def step(s, r, stages):
                if "x" in stages:
                    q = (r + 2) % 4
                    pe.wait_ge(xt_loaded[q], (s + 2 - q) * 4 + 16)
                    if after(s, -1):
                        pe.wait_ge(xt_copied, s + 2)
                    pe.transpose(XT_BANK[:, 0:P], xt_in[q][:, 0:D], ident).then_inc(xt_done, 1)
                if "h" in stages:
                    n = (r + 1) % 2
                    w = pe.value_load(table[0:1, bass.ds(s + (1 + N_SLOTS), 1)], min_val=0,
                                      max_val=(E - 1) * 2 * HID)
                    pe.wait_ge(xt_copied, s + 2)
                    if after(s, 1):
                        pe.wait_ge(gated_ready, s)
                    mm(H1_BANK[n][:, 0:HID], x_t[n][:, :], w13_sb[:, bass.ds(w, HID)], start=True,
                       stop=True).then_inc(h1_done, 1)
                    mm(H3_BANK[n][:, 0:HID], x_t[n][:, :], w13_sb[:, bass.ds(w + HID, HID)], start=True,
                       stop=True).then_inc(h3_done, 1)
                if "t" in stages:
                    pe.wait_ge(gated_ready, s + 1)
                    if after(s, 2):
                        pe.wait_ge(gt_copied, s - 1)
                    for k in range(KT):
                        last = pe.transpose(GT_BANK[r % 2][:, k * P:(k + 1) * P],
                                            gated[r % 2][:, k * P:(k + 1) * P], ident)
                    last.then_inc(gt_done, 1)
                if "y" in stages:
                    n = (r - 1) % 2
                    w = pe.value_load(table[0:1, bass.ds(s + (2 * N_SLOTS - 1), 1)], min_val=0,
                                      max_val=(E - 1) * KT * D)
                    pe.wait_ge(gt_copied, s)
                    if after(s, 2):
                        pe.wait_ge(ye_copied, s - 1)
                    for k in range(KT):
                        last = mm(Y_BANK[:, 0:D], gated_t[n][:, k * P:(k + 1) * P],
                                  w2_sb[:, bass.ds(w + k * D, D)], start=(k == 0), stop=(k == KT - 1))
                    last.then_inc(ye_done, 1)

            over_slots(pe, step)

        @block.scalar
        def _(act):
            act.wait_ge(ld_c, 32)
            act.activation(silu_c[:, :], ct_sb[:, :], ACT.Silu).then_inc(silu_done, 1)

            def modulate(b):
                act.wait_ge(nt_done, b + 1)
                act.activation(h_t[:, W:WIN], M[2][:, 0:S], ACT.Identity, bias=mod_t[:, bass.ds(b + B, 1)],
                               scale=mod_t[:, bass.ds(b, 1)]).then_inc(ht_ready, 1)

            def copy_qk(b, par):
                act.wait_ge(qk_done, b + 1)
                act.activation(q_t[par][:, :], M[2][:, 0:S], ACT.Copy, scale=float(HD) ** -0.5)
                if after(b, 1):
                    act.wait_ge(kdiag_pool, b * 3)
                act.copy(k_sb[:, :], M[2][:, S:2 * S]).then_inc(qk_copied, 1)
                if after(b, 1):
                    act.wait_ge(scores_done, b * 8 - 3)
                for j in range(4):
                    last = act.activation(k_diag[:, 0, j, W:WIN], M[2][:, S:2 * S], ACT.Copy,
                                          scale=headmask[:, 4 * j:4 * j + 1])
                last.then_inc(kdiag_act, 1)

            def copy_v(b, par):
                act.wait_ge(v_done, b + 1)
                if after(b, 2):
                    act.wait_ge(pv_done, b * 8 - 8)
                act.copy(v_lane[par][:, 0:4 * H * LANE].rearrange("p (h e) -> p h e", e=LANE)[:, :, 3 * HD:4 * HD],
                         M[0][:, :].rearrange("p (h e) -> p h e", e=HD)).then_inc(v_copied, 1)

            def softmax(b, i):
                g = b * 8 + i
                pair, quad = i // 4, i % 4
                act.wait_ge(negmax_done, g + 1)
                if after(g, 2):
                    act.wait_ge(pt_done, g - 1)
                if quad == 0 and after(g, 8):
                    act.wait_ge(rden_ready, b * 2 + pair - 1)
                for j in range(4):
                    last = act.activation(probs[i % 2][:, j, :], S_BANK[SCORE_BANK[i]][:, j * P:(j + 1) * P],
                                          ACT.Exp, bias=negmax[:, quad, j:j + 1],
                                          accum_out=den[pair][:, 4 * j + quad:4 * j + quad + 1])
                last.then_inc(probs_done, 1)

            def copy_pay(t, p):
                act.wait_ge(h2_ready, t + 1)
                act.copy(pay[p][:, 1, 0:D], pay[p][:, 0, 0:D]).then_inc(pay_ready, 1)

            def copy_h2t(t, m):
                act.wait_ge(h2t_done, t + 1)
                if after(t, 1):
                    act.wait_ge(gate_done, t)
                act.copy(h2_t[:, :], M[m][:, 0:P]).then_inc(h2t_copied, 1)

            def batch(b, par, first, last):
                for i in range(8):
                    softmax(b, i)
                    if i == 0 and not first:
                        copy_pay(b * 2 - 2, 0)
                    if i == 1 and not first:
                        copy_h2t(b * 2 - 2, 1)
                    if i == 2 and not last:
                        act.wait_ge(v_done, b + 1)
                        modulate(b + 1)
                    if i == 4:
                        if not last:
                            copy_qk(b + 1, 1 - par)
                        if not first:
                            copy_pay(b * 2 - 1, 1)
                    if i == 5 and not last:
                        copy_v(b + 1, 1 - par)
                    if i == 6 and not first:
                        copy_h2t(b * 2 - 1, 2)

            act.wait_ge(mod_done, 2)
            act.wait_ge(zeroed, 2)
            act.wait_ge(ld_x0, 32)
            modulate(0)
            copy_qk(0, 0)
            copy_v(0, 0)
            over_batches(act, batch)
            copy_pay(NT - 2, 0)
            copy_h2t(NT - 2, 1)
            copy_pay(NT - 1, 1)
            copy_h2t(NT - 1, 1)
            act.wait_ge(ex_ready, 1)
            act.activation(ex[:, :], exd[:, :], ACT.Exp).then_inc(ex_ready, 1)

            def step(s, r, stages):
                if "x" in stages:
                    act.wait_ge(xt_done, s + 3)
                    if after(s, 0):
                        act.wait_ge(h3_done, s + 1)
                    act.copy(x_t[r % 2][:, :], XT_BANK[:, 0:P]).then_inc(xt_copied, 1)
                if "h" in stages:
                    n = (r + 1) % 2
                    act.wait_ge(h1_done, s + 2)
                    if after(s, 1):
                        act.wait_ge(gated_ready, s)
                    act.activation(act1[n][:, :], H1_BANK[n][:, 0:HID], ACT.Silu).then_inc(act1_ready, 1)
                if "y" in stages:
                    q = (r - 1) % 4
                    act.wait_ge(ye_done, s)
                    if after(s, 5):
                        act.wait_ge(y_out[q], (s - 1 - q) * 4)
                    act.copy(y_sb[q][:, :], Y_BANK[:, 0:D]).then_inc(ye_copied, 1)

            over_slots(act, step)

        @block.vector
        def _(dve):
            links = counter(dve, "links")

            def link(ins, on_its_own=False):
                ins.then_inc(dve_link, 1)
                dve.reg_add(links, links, 1)
                if on_its_own:
                    dve.wait_ge(ld_x0, 32)
                dve.wait_ge(dve_link, links)

            dve.memset(h_t[:, 0:W], 0.0)
            dve.memset(hot_sum[:, :], 0.0)
            for i in range(2):
                last = dve.memset(gated[i][:, HID:HIDP], 0.0)
            last.then_inc(zeroed, 1)

            def norm_stats(b):
                for p in range(2):
                    last = dve.bn_stats(stats[:, p, :], x_tile(b * 2 + p))
                link(last, on_its_own=True)
                for p in range(2):
                    last = dve.bn_aggr(mv[:, p, :], stats[:, p, :])
                link(last)
                dve.tensor_scalar(veps[:, :], mv[:, :, 1], EPS, None, ALU.add).then_inc(var_ready, 1)

            def norm(b):
                dve.wait_ge(rstd_ready, b + 1)
                if after(b, 1):
                    dve.wait_ge(nt_done, b)
                for p in range(2):
                    last = dve.tensor_scalar(normed[:, p, :], x_tile(b * 2 + p), mv[:, p, 0:1], rstd[:, p:p + 1],
                                             ALU.subtract, ALU.mult)
                last.then_inc(normed_ready, 1)

            dve.wait_ge(ld_x0, 32)
            norm_stats(0)
            dve.wait_ge(mod_mm, 1)
            link(dve.tensor_scalar(mod_t[:, 0:B], M[2][:, 0:B], 1.0, None, ALU.add))
            dve.tensor_copy(mod_t[:, B:2 * B], M[2][:, B:2 * B])
            g_psum = (M[0][0:B, 2 * D:3 * D], M[1][0:B, D:2 * D])
            for k in range(2):
                link(dve.tensor_scalar(mod_a[:, k, :], g_psum[k], -1.0, None, ALU.mult))
                link(dve.tensor_tensor(mod_b[:, k, :], mod_a[:, k, :], g_psum[k], ALU.max))
                link(dve.tensor_scalar(mod_b[:, k, :], mod_b[:, k, :], 0.25, None, ALU.max))
                link(dve.tensor_scalar(mod_a[:, k, :], g_psum[k], 0.0, 2.0, ALU.is_ge, ALU.mult))
                link(dve.scalar_tensor_tensor(out=mod_s[:, 3 * k * D:(3 * k + 1) * D], in0=mod_a[:, k, :],
                                              scalar=-1.0, in1=mod_b[:, k, :], op0=ALU.add, op1=ALU.mult))
            link(dve.tensor_scalar(mod_s[:, D:2 * D], M[1][0:B, 0:D], 1.0, None, ALU.add))
            dve.tensor_copy(mod_s[:, 2 * D:3 * D], M[0][0:B, 3 * D:4 * D]).then_inc(mod_done, 2)
            norm(0)

            def neg_max(b, i):
                dve.wait_ge(scores_done, b * 8 + i + 1)
                dve.tensor_reduce(negmax[:, i % 4, :], S_BANK[SCORE_BANK[i]][:, :].rearrange("p (h k) -> p h k", h=4),
                                  AX_X, ALU.max, negate=True).then_inc(negmax_done, 1)

            def copy_probs_t(g, i):
                dve.wait_ge(pt_done, g + 1)
                if after(g, 2):
                    dve.wait_ge(pv_done, g - 1)
                dve.tensor_copy(probs_t[i % 2][:, :, :].rearrange("p h q -> p (h q)"), PT_BANK[:, :]).then_inc(pt_copied, 1)

            def copy_output(t, p):
                dve.wait_ge(probs_done, t * 4 + 4)
                link(dve.reciprocal(rden[:, :], den[p][:, :]))
                dve.tensor_copy(rden_w[p][:, :, :], rden[:, :].unsqueeze(2).to_broadcast([P, H, HD])).then_inc(rden_ready, 1)
                dve.wait_ge(pv_done, t * 4 + 4)
                dve.tensor_copy(o_sb[:, :], O_BANK[:, 0:P]).then_inc(o_copied, 1)

            def divide_output(t, m):
                dve.wait_ge(rt_done, t + 1)
                dve.wait_ge(o_copied, t + 1)
                dve.tensor_tensor(o_n[:, :], M[m][:, 0:P], o_sb[:, :], ALU.mult).then_inc(on_ready, 1)

            def residual_norm(t, b, p, m):
                dve.wait_ge(y_done, t + 1)
                link(dve.tensor_tensor(yg[:, :], M[m][:, 0:D], mod(b, 0), ALU.mult))
                link(dve.tensor_tensor(x_tile(t), yg[:, :], x_tile(t), ALU.add), on_its_own=True)
                link(dve.bn_stats(stats2[:, :], x_tile(t)), on_its_own=True)
                link(dve.bn_aggr(mv2[:, :], stats2[:, :]))
                dve.tensor_scalar(veps2[:, :], mv2[:, 1:2], EPS, None, ALU.add).then_inc(var2_ready, 1)
                dve.wait_ge(rstd2_ready, t + 1)
                link(dve.tensor_scalar(n2[:, :], x_tile(t), mv2[:, 0:1], rstd2[:, :], ALU.subtract, ALU.mult))
                link(dve.tensor_tensor(n2c[:, :], n2[:, :], mod(b, 1), ALU.mult))
                dve.wait_ge(scattered[p], b * 32 + 16)
                link(dve.tensor_copy(pay[p][:, :, D], cf_("tokid")[:, bass.ds(t * 2, 2)]))
                dve.tensor_tensor(pay[p][:, 0, 0:D], n2c[:, :], mod(b, 2), ALU.add).then_inc(h2_ready, 1)

            def top_two(t, p, m, at):
                dve.wait_ge(gate_done, t + 1)
                link(dve.tensor_copy(sc8[:, :], M[m][:, at:at + E]), on_its_own=True)
                link(dve.max(top8[:, :], sc8[:, :]))
                dve.tensor_copy(top_v[:, bass.ds(t * 2, 2)], top8[:, 0:2])
                link(dve.max_index(ix8[:, :], top8[:, :], sc8[:, :]))
                link(dve.tensor_copy(ixf[:, :], ix8[:, 0:2]))
                for k in range(2):
                    last = dve.tensor_scalar(hot[p][:, k, :], cf_("iota8"), ixf[:, k:k + 1], None, ALU.is_equal)
                link(last)
                dve.tensor_tensor(hot_b[p][:, :], hot[p][:, 0, :], hot[p][:, 1, :], ALU.add).then_inc(hot_ready, 1)

            def choose_rows(t, p, m, at):
                dve.wait_ge(prefix_done, t + 1)
                link(dve.tensor_tensor(pos[:, :], M[m][:, at:at + E], cf_("base8"), ALU.add))
                link(dve.tensor_tensor(junk[:, :, :], hot[p][:, :, :], pos[:, :].unsqueeze(1).to_broadcast([P, 2, E]),
                                       ALU.mult))
                link(dve.tensor_reduce(row_f[:, :], junk[:, :, :], AX_X, ALU.add))
                link(dve.tensor_copy(row_u[p][:, :], row_f[:, :]))
                dve.tensor_tensor(hot_sum[:, :], hot_sum[:, :], hot_b[p][:, :], ALU.add).then_inc(rows_ready, 1)

            def batch(b, par, first, last):
                for i in range(8):
                    copy_probs_t(b * 8 + i, i)
                    if i + 2 < 8:
                        neg_max(b, i + 2)
                    elif not last:
                        neg_max(b + 1, i + 2 - 8)
                    if i == 0:
                        if not last:
                            norm_stats(b + 1)
                        if not first:
                            copy_output(b * 2 - 1, 1)
                        if not last:
                            norm(b + 1)
                    if i == 1 and not first:
                        divide_output(b * 2 - 1, 0)
                    if i == 3 and not first:
                        top_two(b * 2 - 2, 0, 0, D)
                        residual_norm(b * 2 - 1, b - 1, 1, 0)
                    if i == 4:
                        copy_output(b * 2, 0)
                    if i == 5:
                        if not first:
                            choose_rows(b * 2 - 2, 0, 1, P)
                        divide_output(b * 2, 1)
                    if i == 7:
                        if not first:
                            top_two(b * 2 - 1, 1, 1, D)
                        residual_norm(b * 2, b, 0, 1)
                        if not first:
                            choose_rows(b * 2 - 1, 1, 0, 0)

            dve.wait_ge(ld_x, 16)
            dve.wait_ge(mod_in, 16)
            neg_max(0, 0)
            neg_max(0, 1)
            over_batches(dve, batch)
            t = NT - 1
            copy_output(t, 1)
            divide_output(t, 0)
            top_two(t - 1, 0, 2, 0)
            choose_rows(t - 1, 0, 2, 0)
            residual_norm(t, B - 1, 1, 0)
            top_two(t, 1, 2, 0)
            choose_rows(t, 1, 2, 0)

            dve.wait_ge(count_done, 1)
            link(dve.tensor_copy(n_e[:, :], M[1][0:1, 0:E]))
            link(dve.tensor_tensor(cmp_e[:, :, :], n_e[:, :].unsqueeze(2).to_broadcast([1, E, NT]),
                                   cf_("steps", 1).rearrange("p (e j) -> p e j", e=E), ALU.is_gt))
            link(dve.tensor_reduce(tiles_e[:, :], cmp_e[:, :, :], AX_X, ALU.add))
            link(dve.tensor_tensor(cum_m[:, :, :], cf_("tri8", 1).rearrange("p (e f) -> p e f", e=E),
                                   tiles_e[:, :].unsqueeze(1).to_broadcast([1, E, E]), ALU.mult))
            link(dve.tensor_reduce(cum_e[:, :], cum_m[:, :, :], AX_X, ALU.add))
            slot_iota = cf_("slot", 1).rearrange("p (s e) -> p s e", e=E)
            link(dve.tensor_tensor(ge[:, :, :], slot_iota, cum_e[:, :].unsqueeze(1).to_broadcast([1, N_SLOTS, E]),
                                   ALU.is_ge))
            dve.tensor_reduce(slot_e[:, :], ge[:, :, :], AX_X, ALU.add)
            link(dve.tensor_tensor(ge_t[:, :, :], ge[:, :, :], tiles_e[:, :].unsqueeze(1).to_broadcast([1, N_SLOTS, E]),
                                   ALU.mult))
            link(dve.tensor_reduce(slot_b[:, :], ge_t[:, :, :], AX_X, ALU.add))
            link(dve.tensor_tensor(slot_b[:, :], slot_iota[:, :, 0], slot_b[:, :], ALU.subtract))
            link(dve.tensor_scalar(slot_r[:, :], slot_e[:, :], float(REGION), None, ALU.mult))
            link(dve.scalar_tensor_tensor(out=slot_r[:, :], in0=slot_b[:, :], scalar=float(P), in1=slot_r[:, :],
                                          op0=ALU.mult, op1=ALU.add))
            link(dve.tensor_scalar(slot_w[:, :], slot_e[:, :], float(E - 1), None, ALU.min))
            dve.tensor_scalar(table[:, 0:N_SLOTS], slot_r[:, :], float(E * REGION), None, ALU.min)
            dve.tensor_scalar(table[:, N_SLOTS:2 * N_SLOTS], slot_w[:, :], float(2 * HID), None, ALU.mult)
            dve.tensor_scalar(table[:, 2 * N_SLOTS:3 * N_SLOTS], slot_w[:, :], float(KT * D), None, ALU.mult)
            dve.tensor_tensor(table[:, 3 * N_SLOTS:3 * N_SLOTS + E], n_e[:, :], cf_("base8", 1),
                              ALU.add).then_inc(table_ready, 1)
            tv = top_v[:, :].rearrange("p (t k) -> p k t", k=2)
            dve.tensor_tensor(exd[:, :], tv[:, 1, :], tv[:, 0, :], ALU.subtract).then_inc(ex_ready, 1)
            dve.wait_ge(ex_ready, 2)
            link(dve.tensor_scalar(exd[:, :], ex[:, :], 1.0, None, ALU.add))
            link(dve.reciprocal(w_hi[:, :], exd[:, :]))
            link(dve.tensor_tensor(w_lo[:, :], ex[:, :], w_hi[:, :], ALU.mult))

            def step(s, r, stages):
                if "x" in stages:
                    q = (r + 2) % 4
                    dve.wait_ge(xt_loaded[q], (s + 2 - q) * 4 + 16)
                    if after(s, 2):
                        dve.wait_ge(y_out[q], (s + 2 - q) * 4)
                    dve.tensor_copy(ix_u[q][:, :], xt_in[q][:, D:D + 1]).then_inc(ix_ready, 1)
                if "h" in stages:
                    n = (r + 1) % 2
                    dve.wait_ge(h3_done, s + 2)
                    dve.wait_ge(act1_ready, s + 2)
                    if after(s, 1):
                        dve.wait_ge(gt_done, s)
                    dve.tensor_tensor(gated[n][:, 0:HID], H3_BANK[n][:, 0:HID], act1[n][:, :],
                                      ALU.mult).then_inc(gated_ready, 1)
                if "t" in stages:
                    dve.wait_ge(gt_done, s + 1)
                    if after(s, 2):
                        dve.wait_ge(ye_done, s - 1)
                    dve.tensor_copy(gated_t[r % 2][:, :], GT_BANK[r % 2][:, 0:HIDP]).then_inc(gt_copied, 1)

            over_slots(dve, step)

            n = NT // 4
            for i in range(4):
                dve.wait_ge(fin_in[i], 32)
                for t in range(n * i, n * i + n):
                    last = dve.tensor_scalar(fin_b[:, t, :], fin_b[:, t, :], w_lo[:, t:t + 1], None, ALU.mult)
                link(last)
                for t in range(n * i, n * i + n):
                    last = dve.scalar_tensor_tensor(out=fin_b[:, t, :], in0=fin_a[:, t, :], scalar=w_hi[:, t:t + 1],
                                                    in1=fin_b[:, t, :], op0=ALU.mult, op1=ALU.add)
                link(last)
                for b in range(n * i // 2, (n * i + n) // 2):
                    gb = mod(b, 3).unsqueeze(1).to_broadcast([P, 2, D])
                    last = dve.tensor_tensor(fin_b[:, 2 * b:2 * b + 2, :], fin_b[:, 2 * b:2 * b + 2, :], gb, ALU.mult)
                link(last)
                dve.tensor_tensor(fin_a[:, n * i:n * i + n, :], fin_b[:, n * i:n * i + n, :],
                                  x_all[:, n * i:n * i + n, :], ALU.add).then_inc(fin_done, 1)

        @block.gpsimd
        def _(pool):
            tiles, slots = counter(pool, "tiles"), counter(pool, "slots")
            for v in v_lane:
                pool.memset(v[:, :], 0.0)
            pool.memset(k_diag[:, :, :, 0:W].rearrange("p a b w -> p (a b) w"), 0.0).then_inc(zeroed, 1)

            def inv_std(b):
                pool.wait_ge(var_ready, b + 1)
                pool.tensor_tensor(rstd[:, :], veps[:, :], cf_("half"), ALU.pow).then_inc(rstd_ready, 1)

            def inv_std2(t):
                pool.wait_ge(var2_ready, t + 1)
                pool.tensor_tensor(rstd2[:, :], veps2[:, :], cf_("half")[:, 0:1], ALU.pow).then_inc(rstd2_ready, 1)

            def spread_k(b, quad):
                pool.wait_ge(qk_copied, b + 1)
                if after(b, 1):
                    pool.wait_ge(scores_done, b * 8 - 3 + quad)
                pool.tensor_tensor(k_diag[:, quad, :, W:WIN], k_sb[:, :].unsqueeze(1).to_broadcast([P, 4, S]),
                                   headmask.rearrange("p (j q) -> p q j", q=4)[:, quad, :].unsqueeze(2)
                                   .to_broadcast([P, 4, S]), ALU.mult).then_inc(kdiag_pool, 1)

            def scatter(t, p):
                pool.reg_add(tiles, tiles, 1)
                pool.wait_ge(ld_x0, 32)
                pool.wait_ge(rows_ready, tiles)
                pool.wait_ge(pay_ready, tiles)
                for k in range(TOPK):
                    pool.indirect_dma_start(routed[:, :], bass.IndirectOffsetOnAxis(ap=row_u[p][:, k:k + 1], axis=0),
                                            pay[p][:, k, :], None).then_inc(scattered[p], 16)

            def batch(b, par, first, last):
                if not last:
                    inv_std(b + 1)
                if not first:
                    inv_std2(b * 2 - 1)
                if not last:
                    spread_k(b + 1, 1)
                if not first:
                    scatter(b * 2 - 2, 0)
                if not last:
                    spread_k(b + 1, 2)
                inv_std2(b * 2)
                if not last:
                    spread_k(b + 1, 3)
                if not first:
                    scatter(b * 2 - 1, 1)

            pool.wait_ge(ld_x0, 32)
            for p in range(2):
                pool.dma_start(routed[E * REGION + p * W:E * REGION + (p + 1) * W, :],
                               cf_("padrow", W)).then_inc(scattered[p], 16)
            inv_std(0)
            for quad in (1, 2, 3):
                spread_k(0, quad)
            over_batches(pool, batch)
            scatter(NT - 2, 0)
            inv_std2(NT - 1)
            scatter(NT - 1, 1)

            def store(s, q):
                pool.reg_add(slots, slots, 1)
                pool.wait_ge(ld_x0, 32)
                pool.wait_ge(ye_copied, slots)
                pool.wait_ge(ix_ready, slots)
                pool.indirect_dma_start(ranked[:, :], bass.IndirectOffsetOnAxis(ap=ix_u[q][:, 0:1], axis=0),
                                        y_sb[q][:, :], None, bounds_check=TOPK * TOKENS - 1,
                                        oob_is_err=False).then_inc(y_out[q], 16)

            with pool.Fori(0, N_SLOTS // 4) as k:
                for q in range(4):
                    store(k * 4 + q, q)


def constants():
    import numpy as np

    f = np.zeros((P, N_CF), np.float32)
    put = lambda name, a: f.__setitem__((slice(None), slice(*CF[name])), np.broadcast_to(a, (P, CF[name][1] - CF[name][0])))
    row = np.arange(P)[:, None]
    put("ident", np.eye(P))
    put("headmask", row // HD == np.arange(H))
    put("iota8", np.arange(E))
    put("base8", np.arange(E) * REGION)
    put("tokid", np.arange(2 * NT) // 2 * P + row + TOKENS * (np.arange(2 * NT) % 2))
    put("steps", np.tile(np.arange(NT) * P, E))
    put("tri8", (np.arange(E) <= np.arange(E)[:, None]).ravel())
    put("slot", np.repeat(np.arange(N_SLOTS), E))
    put("padrow", np.where(np.arange(PAY) == D, OUT_OF_RANGE, 0.0))
    put("half", -0.5)
    g = np.zeros((P, N_CB), np.float32)
    put = lambda name, a: g.__setitem__((slice(None), slice(*CB[name])), np.reshape(a, (P, -1)))
    put("ident", np.eye(P))
    put("before", row < np.arange(P))
    put("ones", np.ones((P, P)))
    late = np.where(np.arange(W) > row % W, MASKED, 0.0)
    m0 = np.zeros((P, 4, 2 * W))
    m0[:W, :, :W] = MASKED
    m0[:, :, W:] = late[:, None]
    put("mask0", m0)
    put("mask1", np.repeat(late[:, None], 4, 1))
    return f, g.astype(mybir.dt.np(BF16))


def kernel(L0_attn_x, L0_attn_w_qkv, L0_attn_w_out, L0_ffn_Wg, L0_ffn_W1, L0_ffn_W3, L0_ffn_W2, L0_c, L0_wmod):
    import numpy as np
    import concourse.bacc as bacc
    from concourse.bass_utils import run_bass_kernel_spmd

    f, g = constants()
    a = lambda v: np.ascontiguousarray(v)
    w1, w3, w2 = (np.asarray(v) for v in (L0_ffn_W1, L0_ffn_W3, L0_ffn_W2))
    w13 = np.concatenate([w1, w3], axis=1).transpose(2, 0, 1).reshape(P, E * 2 * HID)
    w2t = np.zeros((E, HIDP, D), np.float32)
    w2t[:, :HID] = w2.transpose(0, 2, 1)
    w2t = w2t.reshape(E, KT, P, D).transpose(2, 0, 1, 3).reshape(P, E * KT * D)
    arrays = {
        "x": a(L0_attn_x), "c_t": a(np.asarray(L0_c).T), "wqkv": a(L0_attn_w_qkv), "wout": a(L0_attn_w_out),
        "wmod": a(L0_wmod), "wg_t": a(np.asarray(L0_ffn_Wg).T), "w13": a(w13), "w2": a(w2t), "cf": f, "cb": g,
    }
    nc = bacc.Bacc("TRN2", target_bir_lowering=False, num_devices=1)
    args = {k: nc.dram_tensor(k, v.shape, mybir.dt.from_np(v.dtype), kind="ExternalInput").ap()
            for k, v in arrays.items()}
    out = nc.dram_tensor("out", [B, S, D], F32, kind="ExternalOutput").ap()
    build(nc, out=out, **args)
    r = run_bass_kernel_spmd(nc, [arrays], core_ids=[0])
    return r.results[0]["out"]
```

```python
from contextlib import ExitStack

import concourse.bass as bass
from concourse import mybir

F32 = mybir.dt.float32
BF16 = mybir.dt.bfloat16
I32 = mybir.dt.int32
U32 = mybir.dt.uint32
ALU = mybir.AluOpType
ACT = mybir.ActivationFunctionType
AX_X = mybir.AxisListType.X

P = 128
B, S, D = 8, 256, 128
H, W = 16, 64
HD = D // H
E, TOPK, HID = 8, 2, 352
EPS = 1e-5
NT = B * S // P
TOKENS = B * S
REGION = TOKENS + P
N_ROWS = E * REGION + P
N_SLOTS = -(-(TOPK * TOKENS // P + E - 1) // 4) * 4
PAY = D + 1
HIDP = 384
KT = HIDP // P
WE = 2 * HID + KT * D
LANE = 40
WIN = W + S
OUT_OF_RANGE = 1.0e6
MASKED = -1.0e30

CF = {}
CB = {}


def _columns(table, names):
    at = 0
    for name, n in names:
        table[name] = (at, at + n)
        at += n
    return at


N_CF = _columns(CF, [("ident", P), ("headmask", H), ("iota8", E), ("base8", E), ("tokid", 2 * NT),
                     ("steps", E * NT), ("tri8", E * E), ("slot", N_SLOTS * E), ("padrow", PAY), ("half", NT)])
N_CB = _columns(CB, [("ident", P), ("before", P), ("ones", P), ("region", E), ("mask0", 4 * P), ("mask1", 4 * W)])


def build(nc, x, c_t, wqkv, wout, wmod, wg_t, we, cf, cb, out):
    routed = nc.dram_tensor("routed", [N_ROWS, PAY], F32, kind="Internal").ap()
    ranked = nc.dram_tensor("ranked", [TOPK * TOKENS, D], F32, kind="Internal").ap()
    mod_rows = nc.dram_tensor("mod_rows", [B, 4 * D], F32, kind="Internal").ap()

    with ExitStack() as ctx:
        def sb(name, shape, dt=F32):
            return ctx.enter_context(nc.sbuf_tensor(name, shape, dt))

        def sem(name):
            return ctx.enter_context(nc.semaphore(name))

        bank = [ctx.enter_context(nc.psum_tensor(f"bank{i}", [P, 512], F32)) for i in range(8)]
        S_BANK = bank[0:3]
        PT_BANK = bank[3]
        O_BANK = bank[4]
        M = bank[5:8]
        XT_BANK, H1_BANK, H3_BANK = bank[0], bank[1:3], bank[3:5]
        GT_BANK, Y_BANK = (bank[5], bank[7]), bank[6]

        cf_sb = sb("cf_sb", [P, N_CF])
        cb_sb = sb("cb_sb", [P, N_CB], BF16)
        ct_sb = sb("ct_sb", [P, B])
        wqkv_sb = sb("wqkv_sb", [P, 3 * D])
        wout_sb = sb("wout_sb", [P, D])
        wmod_sb = sb("wmod_sb", [P, 6 * D])
        wg_sb = sb("wg_sb", [P, E])
        we_sb = sb("we_sb", [P, E * WE])
        silu_c = sb("silu_c", [P, B])
        mod_t = sb("mod_t", [P, 2 * B])
        mod_s = sb("mod_s", [B, 4 * D])
        mod_a = sb("mod_a", [B, 2, D])
        mod_b = sb("mod_b", [B, 2, D])
        mod_bc = sb("mod_bc", [P, B * 4 * D])
        x_all = sb("x_all", [P, NT, D])
        stats = sb("stats", [P, NT, 6])
        mv = sb("mv", [P, NT * 2])
        veps = sb("veps", [P, NT])
        rstd = sb("rstd", [P, NT])
        normed = sb("normed", [P, 2, D])
        h_t = sb("h_t", [P, WIN])
        q_t = [sb(f"q_t{i}", [P, S]) for i in range(2)]
        k_sb = sb("k_sb", [P, S])
        k_diag = sb("k_diag", [P, 4, 4, WIN])
        v_lane = [sb(f"v_lane{i}", [P, 4 * H * LANE + LANE]) for i in range(2)]
        negmax = sb("negmax", [P, 4, 4])
        probs = [sb(f"probs{i}", [P, 4, P]) for i in range(2)]
        probs_t = [sb(f"probs_t{i}", [P, 4, P]) for i in range(2)]
        den = [sb(f"den{i}", [P, 2 * H]) for i in range(2)]
        rden = sb("rden", [P, 2 * H])
        rden_w = sb("rden_w", [P, 2 * H, HD])
        o_sb = sb("o_sb", [P, 2, P])
        o_n = sb("o_n", [P, 2, P])
        wout_g = sb("wout_g", [P, D])
        stats2 = sb("stats2", [P, 2, 6])
        mv2 = sb("mv2", [P, 2, 2])
        veps2 = sb("veps2", [P, 2])
        rstd2 = sb("rstd2", [P, 2])
        centred = sb("centred", [P, 2, D])
        pay = [sb(f"pay{i}", [P, 2, TOPK, PAY]) for i in range(2)]
        h2_t = sb("h2_t", [P, 2, P])
        sc8 = sb("sc8", [P, 2, E])
        top8 = sb("top8", [P, 2, 8])
        ix8 = sb("ix8", [P, 2, 8], U32)
        top_v = sb("top_v", [P, NT, TOPK])
        hot = sb("hot", [P, 2, TOPK, E])
        hot_b = sb("hot_b", [P, 2, E], BF16)
        hot_2 = sb("hot_2", [P, E], BF16)
        hot_sum = sb("hot_sum", [P, E], BF16)
        junk = sb("junk", [P, 2, TOPK, E])
        row_u = [sb(f"row_u{i}", [P, 2 * TOPK], U32) for i in range(2)]
        n_e = sb("n_e", [1, E])
        cmp_e = sb("cmp_e", [1, E, NT])
        tiles_e = sb("tiles_e", [1, E])
        cum_m = sb("cum_m", [1, E, E])
        cum_e = sb("cum_e", [1, E])
        ge = sb("ge", [1, N_SLOTS, E])
        ge_t = sb("ge_t", [1, N_SLOTS, E])
        slot_e = sb("slot_e", [1, N_SLOTS])
        slot_b = sb("slot_b", [1, N_SLOTS])
        slot_r = sb("slot_r", [1, N_SLOTS])
        slot_w = sb("slot_w", [1, N_SLOTS])
        table = sb("table", [1, 2 * N_SLOTS + E], I32)
        xt_in = [sb(f"xt_in{i}", [P, PAY]) for i in range(4)]
        ix_u = [sb(f"ix_u{i}", [P, 1], U32) for i in range(4)]
        x_t = [sb(f"x_t{i}", [P, P]) for i in range(2)]
        act1 = [sb(f"act1_{i}", [P, HID]) for i in range(2)]
        gated = [sb(f"gated{i}", [P, HIDP]) for i in range(2)]
        gated_t = [sb(f"gated_t{i}", [P, HIDP]) for i in range(2)]
        y_sb = [sb(f"y_sb{i}", [P, D]) for i in range(4)]
        fin_a = sb("fin_a", [P, NT, D])
        fin_b = sb("fin_b", [P, NT, D])
        ex = sb("ex", [P, NT])
        exd = sb("exd", [P, NT])
        w_hi = sb("w_hi", [P, NT])
        w_lo = sb("w_lo", [P, NT])

        def cf_(name, rows=P):
            a, z = CF[name]
            return cf_sb[0:rows, a:z]

        def cb_(name):
            a, z = CB[name]
            return cb_sb[:, a:z]

        ident, ident_b, headmask = cf_("ident"), cb_("ident"), cf_("headmask")

        def mod(b, which):
            return mod_bc[:, bass.ds((b * 4 + which) * D, D)]

        def x_tile(t):
            return x_all[:, bass.ds(t, 1), :].rearrange("p a d -> p (a d)")

        ld_c = sem("ld_c")
        ld_x0 = sem("ld_x0")
        ld_w = sem("ld_w")
        ld_x = sem("ld_x")
        ld_e = sem("ld_e")
        mod_out = sem("mod_out")
        mod_in = sem("mod_in")
        silu_done = sem("silu_done")
        mod_mm = sem("mod_mm")
        mod_done = sem("mod_done")
        zeroed = sem("zeroed")
        scores_done = sem("scores_done")
        negmax_done = sem("negmax_done")
        probs_done = sem("probs_done")
        pt_done = sem("pt_done")
        pt_copied = sem("pt_copied")
        pv_done = sem("pv_done")
        var_ready = sem("var_ready")
        rstd_ready = sem("rstd_ready")
        normed_ready = sem("normed_ready")
        nt_done = sem("nt_done")
        ht_ready = sem("ht_ready")
        qk_done = sem("qk_done")
        qk_copied = sem("qk_copied")
        kdiag_act = sem("kdiag_act")
        kdiag_pool = sem("kdiag_pool")
        v_done = sem("v_done")
        v_copied = sem("v_copied")
        o_copied = sem("o_copied")
        sums_inverted = sem("sums_inverted")
        rden_ready = sem("rden_ready")
        rt_done = sem("rt_done")
        on_ready = sem("on_ready")
        woutg_ready = sem("woutg_ready")
        y_done = sem("y_done")
        x2_ready = sem("x2_ready")
        stats2_ready = sem("stats2_ready")
        mv2_ready = sem("mv2_ready")
        var2_ready = sem("var2_ready")
        rstd2_ready = sem("rstd2_ready")
        centred_ready = sem("centred_ready")
        h2_ready = sem("h2_ready")
        pay_ready = sem("pay_ready")
        h2t_done = sem("h2t_done")
        h2t_copied = sem("h2t_copied")
        gate_done = sem("gate_done")
        sc8_ready = sem("sc8_ready")
        top8_ready = sem("top8_ready")
        ix8_ready = sem("ix8_ready")
        hot1_ready = sem("hot1_ready")
        hot_ready = sem("hot_ready")
        hot2_ready = sem("hot2_ready")
        prefix_done = sem("prefix_done")
        junk_ready = sem("junk_ready")
        rows_ready = sem("rows_ready")
        scattered = [sem(f"scattered{i}") for i in range(2)]
        dve_link = sem("dve_link")
        count_done = sem("count_done")
        table_ready = sem("table_ready")
        padded = sem("padded")
        xt_loaded = [sem(f"xt_loaded{i}") for i in range(4)]
        xt_done = sem("xt_done")
        xt_copied = sem("xt_copied")
        ix_ready = sem("ix_ready")
        h1_done = sem("h1_done")
        h3_done = sem("h3_done")
        act1_ready = sem("act1_ready")
        gated_ready = sem("gated_ready")
        gt_done = sem("gt_done")
        gt_copied = sem("gt_copied")
        ye_done = sem("ye_done")
        ye_copied = sem("ye_copied")
        y_out = [sem(f"y_out{i}") for i in range(4)]
        fin_in = [sem(f"fin_in{i}") for i in range(4)]
        ex_ready = sem("ex_ready")
        fin_done = sem("fin_done")
        fin_out = sem("fin_out")

        SCORE_BANK = (0, 1, 2, 0, 1, 2, 0, 1)
        SCORE_AGO = (2, 2, 5, 3, 3, 3, 3, 3)

        block = ctx.enter_context(nc.Block())

        def over_batches(eng, body):
            body(0, 0, 0, True, False)
            with eng.Fori(0, B // 2 - 1) as k:
                body(k * 2 + 1, 1, k, False, False)
                body(k * 2 + 2, 0, k + 1, False, False)
            body(B - 1, 1, B // 2 - 1, False, True)

        def counter(eng, name):
            r = eng.alloc_register(f"{name}_count")
            eng.reg_mov(r, 0)
            return r

        @block.sync
        def _(sp):
            xv = x.rearrange("b (a p) d -> p (b a) d", p=P)
            sp.dma_start(ct_sb[:, :], c_t).then_inc(ld_c, 16)
            sp.dma_start(wmod_sb[:, :], wmod).then_inc(ld_c, 16)
            sp.dma_start(x_all[:, 0:2, :], xv[:, 0:2, :]).then_inc(ld_x0, 16)
            sp.dma_start(cf_sb[:, :], cf).then_inc(ld_x0, 16)
            sp.dma_start(wqkv_sb[:, :], wqkv).then_inc(ld_w, 16)
            sp.dma_start(cb_sb[:, :], cb).then_inc(ld_w, 16)
            sp.dma_start(wout_sb[:, :], wout).then_inc(ld_w, 16)
            sp.dma_start(wg_sb[:, :], wg_t).then_inc(ld_w, 16)
            sp.dma_start(x_all[:, 2:NT, :], xv[:, 2:NT, :]).then_inc(ld_x, 16)
            sp.wait_ge(mod_done, 2)
            sp.dma_start(mod_rows, mod_s[:, :]).then_inc(mod_out, 16)
            sp.wait_ge(mod_out, 16)
            sp.dma_start(mod_bc[:, :], mod_rows.rearrange("b n -> (b n)").partition_broadcast(P)).then_inc(mod_in, 16)
            sp.dma_start(we_sb[:, :], we).then_inc(ld_e, 16)

            sp.wait_ge(table_ready, 1)
            for e in range(E):
                row = sp.value_load(table[0:1, 2 * N_SLOTS + e:2 * N_SLOTS + e + 1],
                                    min_val=0, max_val=N_ROWS - P)
                sp.dma_start(routed[bass.ds(row, P), :], cf_("padrow")).then_inc(padded, 16)
            sp.wait_ge(padded, 16 * E)
            for r in scattered:
                sp.wait_ge(r, 16 * NT + 16)

            def load(s, r):
                if not (isinstance(s, int) and s < 4):
                    sp.wait_ge(xt_done, s - 3)
                    sp.wait_ge(ix_ready, s - 3)
                row = sp.value_load(table[0:1, bass.ds(s, 1)], min_val=0, max_val=N_ROWS - P)
                sp.dma_start(xt_in[r][:, :], routed[bass.ds(row, P), :]).then_inc(xt_loaded[r], 16)

            for s in range(4):
                load(s, s)
            with sp.Fori(1, N_SLOTS // 4) as k:
                for r in range(4):
                    load(k * 4 + r, r)

            for r in range(4):
                sp.wait_ge(y_out[r], 16 * (N_SLOTS // 4))
            rv = ranked.rearrange("(k t p) d -> k p t d", k=2, p=P)
            n = NT // 4
            for i in range(4):
                sp.dma_start(fin_a[:, n * i:n * i + n, :], rv[0, :, n * i:n * i + n, :]).then_inc(fin_in[i], 16)
                sp.dma_start(fin_b[:, n * i:n * i + n, :], rv[1, :, n * i:n * i + n, :]).then_inc(fin_in[i], 16)
            ov = out.rearrange("b (a p) d -> p (b a) d", p=P)
            for i in range(4):
                sp.wait_ge(fin_done, i + 1)
                sp.dma_start(ov[:, n * i:n * i + n, :], fin_a[:, n * i:n * i + n, :]).then_inc(fin_out, 16)
            sp.wait_ge(fin_out, 64)

        STAGES = (("x", 2), ("h", 1), ("t", 0), ("y", -1))

        def over_slots(eng, step):
            def at_end(s):
                step(s, s % 4, [c for c, d in STAGES if 0 <= s + d < N_SLOTS])
            for s in range(-2, 5):
                at_end(s)
            with eng.Fori(1, N_SLOTS // 4 - 1) as k:
                for r in range(4):
                    step(k * 4 + (1 + r), (1 + r) % 4, [c for c, _ in STAGES])
            for s in range(N_SLOTS - 3, N_SLOTS + 1):
                at_end(s)

        def after(s, n):
            return not isinstance(s, int) or s >= n

        @block.tensor
        def _(pe):
            mm = pe.matmul
            pe.wait_ge(ld_c, 32)
            pe.wait_ge(silu_done, 1)
            mm(M[0][0:B, :], silu_c[:, :], wmod_sb[:, 0:512], start=True, stop=True)
            mm(M[1][0:B, 0:256], silu_c[:, :], wmod_sb[:, 512:768], start=True, stop=True)
            mm(M[2][:, 0:B], wmod_sb[:, D:2 * D], silu_c[:, :], start=True, stop=True)
            mm(M[2][:, B:2 * B], wmod_sb[:, 0:D], silu_c[:, :], start=True, stop=True).then_inc(mod_mm, 1)

            def norm_t(b):
                pe.wait_ge(normed_ready, b + 1)
                pe.transpose(M[2][:, 0:P], normed[:, 0, :], ident)
                pe.transpose(M[2][:, P:2 * P], normed[:, 1, :], ident).then_inc(nt_done, 1)

            def project_qk(b):
                pe.wait_ge(ht_ready, b + 1)
                mm(M[2][:, 0:S], wqkv_sb[:, 0:D], h_t[:, W:WIN], start=True, stop=True)
                mm(M[2][:, S:2 * S], wqkv_sb[:, D:2 * D], h_t[:, W:WIN], start=True, stop=True).then_inc(qk_done, 1)

            def project_v():
                for c in range(4):
                    last = mm(M[0][:, c * P:(c + 1) * P], h_t[:, c * W:c * W + 2 * W], wqkv_sb[:, 2 * D:3 * D],
                              start=True, stop=True)
                last.then_inc(v_done, 1)

            def scores(b, par, i):
                g = b * 8 + i
                pair, quad = i // 4, i % 4
                if i == 0:
                    pe.wait_ge(qk_copied, b + 1)
                    pe.wait_ge(kdiag_act, b + 1)
                if 0 < i < 4:
                    pe.wait_ge(kdiag_pool, b * 3 + quad)
                if after(g, 3):
                    pe.wait_ge(probs_done, g + 1 - SCORE_AGO[i])
                s_bank = S_BANK[SCORE_BANK[i]]
                sv = s_bank[:, :].rearrange("p (h k) -> p h k", h=4)
                if pair == 0:
                    mm(s_bank[:, :], ident_b, cb_("mask0"), start=True, stop=False, skip_group_check=True)
                else:
                    mm(sv[:, :, W:2 * W], ident_b, cb_("mask1").rearrange("p (h k) -> p h k", h=4),
                       start=True, stop=False, skip_group_check=True)
                for a in range(2):
                    c = 2 * pair + a
                    last = mm(sv[a * W:(a + 1) * W, :, :], q_t[par][:, c * W:(c + 1) * W],
                              k_diag[:, quad, :, c * W:c * W + 2 * W], start=False, stop=True,
                              skip_group_check=True)
                last.then_inc(scores_done, 1)

            def probs_transpose(g, i):
                pe.wait_ge(probs_done, g + 1)
                if after(g, 1):
                    pe.wait_ge(pt_copied, g)
                for j in range(4):
                    last = pe.transpose(PT_BANK[:, j * P:(j + 1) * P], probs[i % 2][:, j, :], ident)
                last.then_inc(pt_done, 1)

            def pv(b, par, i):
                pair, quad = i // 4, i % 4
                pe.wait_ge(pt_copied, b * 8 + i + 1)
                if i == 0:
                    pe.wait_ge(v_copied, b + 1)
                if quad == 0 and after(b * 8 + i, 1):
                    pe.wait_ge(o_copied, b * 2 + pair)
                for a in range(2):
                    c = 2 * pair + a
                    for j in range(4):
                        at = (c * H + 4 * j + quad) * LANE + 3 * HD - quad * HD
                        last = mm(O_BANK[32 * j:32 * j + 32, a * W:(a + 1) * W], v_lane[par][:, at:at + 32],
                                  probs_t[i % 2][:, j, a * W:(a + 1) * W], start=(quad == 0 and a == 0),
                                  stop=(quad == 3), skip_group_check=True)
                last.then_inc(pv_done, 1)

            def rden_t(e, m):
                pe.wait_ge(rden_ready, e + 1)
                for p in range(2):
                    last = pe.transpose(M[m][:, p * P:(p + 1) * P],
                                        rden_w[:, p * H:(p + 1) * H, :].rearrange("p h d -> p (h d)"), ident)
                last.then_inc(rt_done, 1)

            def out_project(e, m):
                pe.wait_ge(on_ready, e + 1)
                pe.wait_ge(woutg_ready, e + 1)
                for p in range(2):
                    last = mm(M[m][:, p * D:(p + 1) * D], o_n[:, p, :], wout_g[:, :], start=True, stop=True)
                last.then_inc(y_done, 1)

            def h2_transpose(e, par, m):
                pe.wait_ge(h2_ready, e + 1)
                for p in range(2):
                    last = pe.transpose(M[m][:, p * P:(p + 1) * P], pay[par][:, p, 0, 0:D], ident)
                last.then_inc(h2t_done, 1)

            def gate(e, m):
                pe.wait_ge(h2t_copied, e + 1)
                for p in range(2):
                    last = mm(M[m][:, p * E:(p + 1) * E], h2_t[:, p, :], wg_sb[:, :], start=True, stop=True,
                              skip_group_check=True)
                last.then_inc(gate_done, 1)

            def prefix(e, m):
                pe.wait_ge(hot_ready, e + 1)
                for p in range(2):
                    at = M[m][:, p * E:(p + 1) * E]
                    mm(at, cb_("before"), hot_b[:, p, :], start=True, stop=False, skip_group_check=True)
                    if p:
                        mm(at, cb_("ones"), hot_b[:, 0, :], start=False, stop=False, skip_group_check=True)
                    last = mm(at, cb_("ones"), hot_sum[:, :], start=False, stop=True, skip_group_check=True)
                last.then_inc(prefix_done, 1)

            def spare(b, par, i, first, last):
                if i == 0 and not first:
                    pe.wait_ge(v_copied, b + 1)
                    rden_t(b - 1, 0)
                if i == 1:
                    if not first:
                        out_project(b - 1, 1)
                    if not last:
                        norm_t(b + 1)
                if i == 3 and not last:
                    project_qk(b + 1)
                if i == 4 and not first:
                    h2_transpose(b - 1, 1 - par, 0)
                if i == 5:
                    if not first:
                        gate(b - 1, 1)
                    if not last:
                        if first:
                            pe.wait_ge(v_copied, 1)
                        project_v()
                if i == 7 and not first:
                    prefix(b - 1, 1)

            def batch(b, par, half, first, last):
                for i in range(8):
                    if i + 2 < 8:
                        scores(b, par, i + 2)
                    elif not last:
                        scores(b + 1, 1 - par, i + 2 - 8)
                    probs_transpose(b * 8 + i, i)
                    if i > 0:
                        pv(b, par, i - 1)
                    elif not first:
                        pv(b - 1, 1 - par, 7)
                    spare(b, par, i, first, last)

            pe.wait_ge(mod_done, 2)
            pe.wait_ge(ld_x0, 32)
            pe.wait_ge(ld_w, 64)
            norm_t(0)
            project_qk(0)
            project_v()
            scores(0, 0, 0)
            scores(0, 0, 1)
            over_batches(pe, batch)
            pv(B - 1, 1, 7)
            rden_t(B - 1, 0)
            out_project(B - 1, 1)
            h2_transpose(B - 1, 1, 0)
            gate(B - 1, 1)
            prefix(B - 1, 1)
            pe.wait_ge(rows_ready, B)
            mm(M[2][:, 0:E], cb_("ones"), hot_sum[:, :], start=True, stop=True).then_inc(count_done, 1)

            pe.wait_ge(ld_e, 16)
            pe.wait_ge(table_ready, 1)

            w_at = [pe.alloc_register(f"w_at{q}") for q in range(4)]

            def weights(q, at, n):
                w = pe.snap(w_at[q], min_val=0, max_val=(E - 1) * WE)
                return we_sb[:, bass.ds(w + at, n)]

            def step(s, r, stages):
                if "h" in stages:
                    n = (r + 1) % 2
                    pe.wait_ge(xt_copied, s + 2)
                    if after(s, 1):
                        pe.wait_ge(gated_ready, s)
                    mm(H1_BANK[n][:, 0:HID], x_t[n][:, :], weights((r + 1) % 4, 0, HID), start=True,
                       stop=True).then_inc(h1_done, 1)
                    mm(H3_BANK[n][:, 0:HID], x_t[n][:, :], weights((r + 1) % 4, HID, HID), start=True,
                       stop=True).then_inc(h3_done, 1)
                if "x" in stages:
                    q = (r + 2) % 4
                    pe.reg_load(w_at[q], table[0:1, bass.ds(s + (2 + N_SLOTS), 1)])
                    pe.wait_ge(xt_loaded[q], (s + 2 - q) * 4 + 16)
                    if after(s, -1):
                        pe.wait_ge(xt_copied, s + 2)
                    pe.transpose(XT_BANK[:, 0:P], xt_in[q][:, 0:D], ident).then_inc(xt_done, 1)
                if "t" in stages:
                    pe.wait_ge(gated_ready, s + 1)
                    if after(s, 2):
                        pe.wait_ge(gt_copied, s - 1)
                    for k in range(KT):
                        last = pe.transpose(GT_BANK[r % 2][:, k * P:(k + 1) * P],
                                            gated[r % 2][:, k * P:(k + 1) * P], ident)
                    last.then_inc(gt_done, 1)
                if "y" in stages:
                    n = (r - 1) % 2
                    pe.wait_ge(gt_copied, s)
                    if after(s, 2):
                        pe.wait_ge(ye_copied, s - 1)
                    for k in range(KT):
                        last = mm(Y_BANK[:, 0:D], gated_t[n][:, k * P:(k + 1) * P],
                                  weights((r - 1) % 4, 2 * HID + k * D, D), start=(k == 0), stop=(k == KT - 1))
                    last.then_inc(ye_done, 1)

            over_slots(pe, step)

        @block.scalar
        def _(act):
            act.wait_ge(ld_c, 32)
            act.activation(silu_c[:, :], ct_sb[:, :], ACT.Silu).then_inc(silu_done, 1)

            def modulate(b):
                act.wait_ge(nt_done, b + 1)
                act.activation(h_t[:, W:WIN], M[2][:, 0:S], ACT.Identity, bias=mod_t[:, bass.ds(b + B, 1)],
                               scale=mod_t[:, bass.ds(b, 1)]).then_inc(ht_ready, 1)

            def copy_qk(b, par):
                act.wait_ge(qk_done, b + 1)
                act.activation(q_t[par][:, :], M[2][:, 0:S], ACT.Copy, scale=float(HD) ** -0.5)
                if after(b, 1):
                    act.wait_ge(kdiag_pool, b * 3)
                act.copy(k_sb[:, :], M[2][:, S:2 * S]).then_inc(qk_copied, 1)

            def spread_k(b):
                if after(b, 1):
                    act.wait_ge(scores_done, b * 8 - 3)
                for j in range(4):
                    last = act.activation(k_diag[:, 0, j, W:WIN], M[2][:, S:2 * S], ACT.Copy,
                                          scale=headmask[:, 4 * j:4 * j + 1])
                last.then_inc(kdiag_act, 1)

            def copy_v(b, par):
                act.wait_ge(v_done, b + 1)
                if after(b, 2):
                    act.wait_ge(pv_done, b * 8 - 8)
                act.copy(v_lane[par][:, 0:4 * H * LANE].rearrange("p (h e) -> p h e", e=LANE)[:, :, 3 * HD:4 * HD],
                         M[0][:, :].rearrange("p (h e) -> p h e", e=HD)).then_inc(v_copied, 1)

            def softmax(b, par, i):
                g = b * 8 + i
                pair, quad = i // 4, i % 4
                act.wait_ge(negmax_done, g + 1)
                if after(g, 2):
                    act.wait_ge(pt_done, g - 1)
                for j in range(4):
                    h = pair * H + 4 * j + quad
                    last = act.activation(probs[i % 2][:, j, :], S_BANK[SCORE_BANK[i]][:, j * P:(j + 1) * P],
                                          ACT.Exp, bias=negmax[:, quad, j:j + 1], accum_out=den[par][:, h:h + 1])
                last.then_inc(probs_done, 1)

            def copy_pay(e, par):
                act.wait_ge(h2_ready, e + 1)
                act.copy(pay[par][:, :, 1, 0:D], pay[par][:, :, 0, 0:D]).then_inc(pay_ready, 1)

            def copy_h2t(e, m):
                act.wait_ge(h2t_done, e + 1)
                act.copy(h2_t[:, :, :].rearrange("p a d -> p (a d)"), M[m][:, 0:2 * P]).then_inc(h2t_copied, 1)

            def batch(b, par, half, first, last):
                for i in range(8):
                    softmax(b, par, i)
                    if i == 2 and not last:
                        act.wait_ge(v_done, b + 1)
                        modulate(b + 1)
                    if i == 4:
                        if not last:
                            copy_qk(b + 1, 1 - par)
                        if not first:
                            copy_pay(b - 1, 1 - par)
                    if i == 5:
                        if not first:
                            copy_h2t(b - 1, 0)
                        if not last:
                            spread_k(b + 1)
                    if i == 6 and not last:
                        copy_v(b + 1, 1 - par)

            act.wait_ge(mod_done, 2)
            act.wait_ge(zeroed, 2)
            act.wait_ge(ld_x0, 32)
            modulate(0)
            copy_qk(0, 0)
            spread_k(0)
            copy_v(0, 0)
            over_batches(act, batch)
            copy_h2t(B - 1, 0)
            copy_pay(B - 1, 1)
            act.wait_ge(ex_ready, 1)
            act.activation(ex[:, :], exd[:, :], ACT.Exp).then_inc(ex_ready, 1)

            def step(s, r, stages):
                if "h" in stages:
                    n = (r + 1) % 2
                    act.wait_ge(h1_done, s + 2)
                    if after(s, 1):
                        act.wait_ge(gated_ready, s)
                    act.activation(act1[n][:, :], H1_BANK[n][:, 0:HID], ACT.Silu).then_inc(act1_ready, 1)
                if "x" in stages:
                    act.wait_ge(xt_done, s + 3)
                    if after(s, 0):
                        act.wait_ge(h3_done, s + 1)
                    act.copy(x_t[r % 2][:, :], XT_BANK[:, 0:P]).then_inc(xt_copied, 1)
                if "y" in stages:
                    q = (r - 1) % 4
                    act.wait_ge(ye_done, s)
                    if after(s, 5):
                        act.wait_ge(y_out[q], (s - 1 - q) * 4)
                    act.copy(y_sb[q][:, :], Y_BANK[:, 0:D]).then_inc(ye_copied, 1)

            over_slots(act, step)

        @block.vector
        def _(dve):
            links = counter(dve, "links")

            def link(ins, on_its_own=False):
                ins.then_inc(dve_link, 1)
                dve.reg_add(links, links, 1)
                if on_its_own:
                    dve.wait_ge(ld_x0, 32)
                dve.wait_ge(dve_link, links)

            dve.memset(h_t[:, 0:W], 0.0)
            for i in range(2):
                last = dve.memset(gated[i][:, HID:HIDP], 0.0)
            last.then_inc(zeroed, 1)

            def norm_stats(t, n):
                for i in range(t, t + n):
                    last = dve.bn_stats(stats[:, i, :], x_all[:, i, :])
                link(last, on_its_own=True)
                for i in range(t, t + n):
                    last = dve.bn_aggr(mv[:, 2 * i:2 * i + 2], stats[:, i, :])
                link(last)
                return dve.tensor_scalar(veps[:, t:t + n], mv[:, :].rearrange("p (t k) -> p t k", k=2)[:, t:t + n, 1],
                                         EPS, None, ALU.add)

            def norm(b):
                for p in range(2):
                    t = b * 2 + p
                    last = dve.tensor_scalar(normed[:, p, :], x_tile(t), mv[:, bass.ds(t * 2, 1)],
                                             rstd[:, bass.ds(t, 1)], ALU.subtract, ALU.mult)
                last.then_inc(normed_ready, 1)

            dve.wait_ge(ld_x0, 32)
            norm_stats(0, 2).then_inc(var_ready, 1)
            dve.wait_ge(mod_mm, 1)
            link(dve.tensor_scalar(mod_t[:, 0:B], M[2][:, 0:B], 1.0, None, ALU.add))
            dve.tensor_copy(mod_t[:, B:2 * B], M[2][:, B:2 * B])
            g_psum = (M[0][0:B, 2 * D:3 * D], M[1][0:B, D:2 * D])
            for k in range(2):
                link(dve.tensor_scalar(mod_a[:, k, :], g_psum[k], -1.0, None, ALU.mult))
                link(dve.tensor_tensor(mod_b[:, k, :], mod_a[:, k, :], g_psum[k], ALU.max))
                link(dve.tensor_scalar(mod_b[:, k, :], mod_b[:, k, :], 0.25, None, ALU.max))
                link(dve.tensor_scalar(mod_a[:, k, :], g_psum[k], 0.0, 2.0, ALU.is_ge, ALU.mult))
                link(dve.scalar_tensor_tensor(out=mod_s[:, 3 * k * D:(3 * k + 1) * D], in0=mod_a[:, k, :],
                                              scalar=-1.0, in1=mod_b[:, k, :], op0=ALU.add, op1=ALU.mult))
            link(dve.tensor_scalar(mod_s[:, D:2 * D], M[1][0:B, 0:D], 1.0, None, ALU.add))
            dve.tensor_copy(mod_s[:, 2 * D:3 * D], M[0][0:B, 3 * D:4 * D]).then_inc(mod_done, 2)
            dve.wait_ge(rstd_ready, 1)
            norm(0)

            def neg_max(b, i):
                dve.wait_ge(scores_done, b * 8 + i + 1)
                dve.tensor_reduce(negmax[:, i % 4, :], S_BANK[SCORE_BANK[i]][:, :].rearrange("p (h k) -> p h k", h=4),
                                  AX_X, ALU.max, negate=True).then_inc(negmax_done, 1)

            def copy_probs_t(g, i):
                dve.wait_ge(pt_done, g + 1)
                if after(g, 2):
                    dve.wait_ge(pv_done, g - 1)
                dve.tensor_copy(probs_t[i % 2][:, :, :].rearrange("p h q -> p (h q)"), PT_BANK[:, :]).then_inc(pt_copied, 1)

            finish = counter(dve, "finish")

            def wait_alone(sem_):
                dve.wait_ge(ld_x0, 32)
                dve.wait_ge(sem_, finish)

            def copy_output(b, p):
                dve.wait_ge(pv_done, b * 8 + 4 * p + 4)
                dve.tensor_copy(o_sb[:, p, :], O_BANK[:, 0:P]).then_inc(o_copied, 1)

            def invert_sums(par):
                dve.reciprocal(rden[:, :], den[par][:, :]).then_inc(sums_inverted, 1)

            def widen_sums():
                dve.wait_ge(sums_inverted, finish)
                dve.tensor_copy(rden_w[:, :, :], rden[:, :].unsqueeze(2).to_broadcast([P, 2 * H, HD])).then_inc(rden_ready, 1)

            def divide_output(e):
                dve.wait_ge(rt_done, finish)
                dve.wait_ge(o_copied, e * 2 + 2)
                dve.tensor_tensor(o_n[:, :, :].rearrange("p a d -> p (a d)"), M[0][:, 0:2 * P],
                                  o_sb[:, :, :].rearrange("p a d -> p (a d)"), ALU.mult).then_inc(on_ready, 1)

            def add_residual(e):
                dve.wait_ge(y_done, finish)
                x2 = x_all[:, bass.ds(e * 2, 2), :]
                dve.tensor_tensor(x2, M[1][:, 0:2 * D].rearrange("p (a d) -> p a d", a=2), x2,
                                  ALU.add).then_inc(x2_ready, 1)

            def stats_2(e):
                wait_alone(x2_ready)
                for p in range(2):
                    last = dve.bn_stats(stats2[:, p, :], x_tile(e * 2 + p))
                last.then_inc(stats2_ready, 1)

            def aggregate_2():
                wait_alone(stats2_ready)
                for p in range(2):
                    last = dve.bn_aggr(mv2[:, p, :], stats2[:, p, :])
                last.then_inc(mv2_ready, 1)

            def variance_2():
                dve.wait_ge(mv2_ready, finish)
                dve.tensor_scalar(veps2[:, :], mv2[:, :, 1], EPS, None, ALU.add).then_inc(var2_ready, 1)

            def centre_2(e):
                for p in range(2):
                    last = dve.scalar_tensor_tensor(out=centred[:, p, :], in0=x_tile(e * 2 + p), scalar=mv2[:, p, 0:1],
                                                    in1=mod(e, 1), op0=ALU.subtract, op1=ALU.mult)
                last.then_inc(centred_ready, 1)

            def modulate_2(e, par, half):
                dve.wait_ge(scattered[par], half * 64 + 16)
                dve.tensor_copy(pay[par][:, :, :, D],
                                cf_("tokid")[:, bass.ds(e * 4, 4)].rearrange("p (a k) -> p a k", a=2))
                dve.wait_ge(rstd2_ready, finish)
                dve.wait_ge(centred_ready, finish)
                for p in range(2):
                    last = dve.scalar_tensor_tensor(out=pay[par][:, p, 0, 0:D], in0=centred[:, p, :],
                                                    scalar=rstd2[:, p:p + 1], in1=mod(e, 2), op0=ALU.mult,
                                                    op1=ALU.add)
                last.then_inc(h2_ready, 1)

            def copy_scores():
                dve.wait_ge(gate_done, finish)
                dve.tensor_copy(sc8[:, :, :].rearrange("p a e -> p (a e)"), M[1][:, 0:2 * E]).then_inc(sc8_ready, 1)

            def top_scores():
                wait_alone(sc8_ready)
                for p in range(2):
                    last = dve.max(top8[:, p, :], sc8[:, p, :])
                last.then_inc(top8_ready, 1)

            def top_experts(e):
                wait_alone(top8_ready)
                for p in range(2):
                    last = dve.max_index(ix8[:, p, :], top8[:, p, :], sc8[:, p, :])
                last.then_inc(ix8_ready, 1)
                dve.tensor_copy(top_v[:, bass.ds(e * 2, 2), :], top8[:, :, 0:TOPK])

            def one_hot():
                dve.wait_ge(ix8_ready, finish)
                for p in range(2):
                    last = dve.tensor_tensor(hot[:, p, :, :], ix8[:, p, 0:TOPK].unsqueeze(2).to_broadcast([P, TOPK, E]),
                                             cf_("iota8").unsqueeze(1).to_broadcast([P, TOPK, E]), ALU.is_equal)
                last.then_inc(hot1_ready, 1)

            def sum_ranks():
                dve.wait_ge(hot1_ready, finish)
                dve.tensor_tensor(hot_b[:, :, :], hot[:, :, 0, :], hot[:, :, 1, :], ALU.add).then_inc(hot_ready, 1)

            def sum_tiles():
                dve.wait_ge(hot_ready, finish)
                dve.tensor_tensor(hot_2[:, :], hot_b[:, 0, :], hot_b[:, 1, :], ALU.add).then_inc(hot2_ready, 1)

            def choose_rows(par):
                dve.wait_ge(prefix_done, finish)
                for p in range(2):
                    last = dve.tensor_tensor(junk[:, p, :, :], hot[:, p, :, :],
                                             M[1][:, p * E:(p + 1) * E].unsqueeze(1).to_broadcast([P, TOPK, E]), ALU.mult)
                last.then_inc(junk_ready, 1)
                dve.wait_ge(hot2_ready, finish)
                dve.tensor_tensor(hot_sum[:, :], hot_sum[:, :], hot_2[:, :], ALU.add)
                dve.wait_ge(junk_ready, finish)
                with nc.allow_low_precision(reason="one term of a sum is not zero, and whole"):
                    dve.tensor_reduce(row_u[par][:, :], junk[:, :, :, :].rearrange("p a k e -> p (a k) e"), AX_X,
                                      ALU.add).then_inc(rows_ready, 1)

            def batch(b, par, half, first, last):
                e, epar = b - 1, 1 - par
                ehalf = half if par else half - 1
                if not first:
                    dve.reg_add(finish, finish, 1)
                for i in range(8):
                    if not first:
                        if i == 0:
                            widen_sums()
                        if i == 1:
                            divide_output(e)
                        if i == 2:
                            add_residual(e)
                        if i == 3:
                            variance_2()
                        if i == 6:
                            top_scores()
                        if i == 7:
                            sum_ranks()
                    copy_probs_t(b * 8 + i, i)
                    if i == 0 and not last:
                        dve.wait_ge(rstd_ready, 2 if first else 3)
                        dve.wait_ge(nt_done, b + 1)
                        norm(b + 1)
                    if not first:
                        if i == 2:
                            stats_2(e)
                        if i == 3:
                            centre_2(e)
                        if i == 6:
                            top_experts(e)
                    if i == 7:
                        if not first:
                            sum_tiles()
                        invert_sums(par)
                    if i + 2 < 8:
                        neg_max(b, i + 2)
                    elif not last:
                        neg_max(b + 1, i + 2 - 8)
                    if first and 1 <= i < 7:
                        done = norm_stats(2 + 2 * i, 2)
                        if i == 6:
                            done.then_inc(var_ready, 1)
                    if i == 4:
                        copy_output(b, 0)
                    if not first:
                        if i == 0:
                            copy_output(e, 1)
                        if i == 2:
                            aggregate_2()
                        if i == 3:
                            modulate_2(e, epar, ehalf)
                        if i == 5:
                            copy_scores()
                        if i == 6:
                            one_hot()
                        if i == 7:
                            choose_rows(epar)

            dve.wait_ge(ld_x, 16)
            norm_stats(2, 2).then_inc(var_ready, 1)
            dve.wait_ge(ld_w, 64)
            dve.tensor_copy(hot_sum[:, :], cb_("region"))
            neg_max(0, 0)
            neg_max(0, 1)
            dve.wait_ge(mod_in, 16)
            over_batches(dve, batch)
            dve.reg_add(finish, finish, 1)
            e = B - 1
            widen_sums()
            copy_output(e, 1)
            divide_output(e)
            add_residual(e)
            stats_2(e)
            aggregate_2()
            variance_2()
            centre_2(e)
            modulate_2(e, 1, e // 2)
            copy_scores()
            top_scores()
            top_experts(e)
            one_hot()
            sum_ranks()
            sum_tiles()
            choose_rows(1)

            dve.wait_ge(count_done, 1)
            link(dve.tensor_tensor(n_e[:, :], M[2][0:1, 0:E], cf_("base8", 1), ALU.subtract))
            link(dve.tensor_tensor(cmp_e[:, :, :], n_e[:, :].unsqueeze(2).to_broadcast([1, E, NT]),
                                   cf_("steps", 1).rearrange("p (e j) -> p e j", e=E), ALU.is_gt))
            link(dve.tensor_reduce(tiles_e[:, :], cmp_e[:, :, :], AX_X, ALU.add))
            link(dve.tensor_tensor(cum_m[:, :, :], cf_("tri8", 1).rearrange("p (e f) -> p e f", e=E),
                                   tiles_e[:, :].unsqueeze(1).to_broadcast([1, E, E]), ALU.mult))
            link(dve.tensor_reduce(cum_e[:, :], cum_m[:, :, :], AX_X, ALU.add))
            slot_iota = cf_("slot", 1).rearrange("p (s e) -> p s e", e=E)
            link(dve.tensor_tensor(ge[:, :, :], slot_iota, cum_e[:, :].unsqueeze(1).to_broadcast([1, N_SLOTS, E]),
                                   ALU.is_ge))
            dve.tensor_reduce(slot_e[:, :], ge[:, :, :], AX_X, ALU.add)
            link(dve.tensor_tensor(ge_t[:, :, :], ge[:, :, :], tiles_e[:, :].unsqueeze(1).to_broadcast([1, N_SLOTS, E]),
                                   ALU.mult))
            link(dve.tensor_reduce(slot_b[:, :], ge_t[:, :, :], AX_X, ALU.add))
            link(dve.tensor_tensor(slot_b[:, :], slot_iota[:, :, 0], slot_b[:, :], ALU.subtract))
            link(dve.tensor_scalar(slot_r[:, :], slot_e[:, :], float(REGION), None, ALU.mult))
            link(dve.scalar_tensor_tensor(out=slot_r[:, :], in0=slot_b[:, :], scalar=float(P), in1=slot_r[:, :],
                                          op0=ALU.mult, op1=ALU.add))
            link(dve.tensor_scalar(slot_w[:, :], slot_e[:, :], float(E - 1), None, ALU.min))
            dve.tensor_scalar(table[:, 0:N_SLOTS], slot_r[:, :], float(E * REGION), None, ALU.min)
            dve.tensor_scalar(table[:, N_SLOTS:2 * N_SLOTS], slot_w[:, :], float(WE), None, ALU.mult)
            dve.tensor_copy(table[:, 2 * N_SLOTS:2 * N_SLOTS + E], M[2][0:1, 0:E]).then_inc(table_ready, 1)
            dve.tensor_tensor(exd[:, :], top_v[:, :, 1], top_v[:, :, 0], ALU.subtract).then_inc(ex_ready, 1)
            dve.wait_ge(ex_ready, 2)
            link(dve.tensor_scalar(exd[:, :], ex[:, :], 1.0, None, ALU.add))
            link(dve.reciprocal(w_hi[:, :], exd[:, :]))
            link(dve.tensor_tensor(w_lo[:, :], ex[:, :], w_hi[:, :], ALU.mult))

            def step(s, r, stages):
                if "h" in stages:
                    n = (r + 1) % 2
                    dve.wait_ge(h3_done, s + 2)
                    dve.wait_ge(act1_ready, s + 2)
                    if after(s, 1):
                        dve.wait_ge(gt_done, s)
                    dve.tensor_tensor(gated[n][:, 0:HID], H3_BANK[n][:, 0:HID], act1[n][:, :],
                                      ALU.mult).then_inc(gated_ready, 1)
                if "h" in stages:
                    q = (r + 1) % 4
                    dve.wait_ge(xt_loaded[q], (s + 1 - q) * 4 + 16)
                    if after(s, 3):
                        dve.wait_ge(y_out[q], (s + 1 - q) * 4)
                    dve.tensor_copy(ix_u[q][:, :], xt_in[q][:, D:D + 1]).then_inc(ix_ready, 1)
                if "t" in stages:
                    dve.wait_ge(gt_done, s + 1)
                    if after(s, 2):
                        dve.wait_ge(ye_done, s - 1)
                    dve.tensor_copy(gated_t[r % 2][:, :], GT_BANK[r % 2][:, 0:HIDP]).then_inc(gt_copied, 1)

            over_slots(dve, step)

            n = NT // 4
            for i in range(4):
                dve.wait_ge(fin_in[i], 32)
                for t in range(n * i, n * i + n):
                    last = dve.tensor_scalar(fin_b[:, t, :], fin_b[:, t, :], w_lo[:, t:t + 1], None, ALU.mult)
                link(last)
                for t in range(n * i, n * i + n):
                    last = dve.scalar_tensor_tensor(out=fin_b[:, t, :], in0=fin_a[:, t, :], scalar=w_hi[:, t:t + 1],
                                                    in1=fin_b[:, t, :], op0=ALU.mult, op1=ALU.add)
                link(last)
                for b in range(n * i // 2, (n * i + n) // 2):
                    gb = mod(b, 3).unsqueeze(1).to_broadcast([P, 2, D])
                    last = dve.tensor_tensor(fin_b[:, 2 * b:2 * b + 2, :], fin_b[:, 2 * b:2 * b + 2, :], gb, ALU.mult)
                link(last)
                dve.tensor_tensor(fin_a[:, n * i:n * i + n, :], fin_b[:, n * i:n * i + n, :],
                                  x_all[:, n * i:n * i + n, :], ALU.add).then_inc(fin_done, 1)

        @block.gpsimd
        def _(pool):
            batches, slots = counter(pool, "batches"), counter(pool, "slots")
            for v in v_lane:
                pool.memset(v[:, :], 0.0)
            pool.memset(k_diag[:, :, :, 0:W].rearrange("p a b w -> p (a b) w"), 0.0).then_inc(zeroed, 1)

            def inv_std(count, t, n):
                pool.wait_ge(var_ready, count)
                pool.tensor_tensor(rstd[:, t:t + n], veps[:, t:t + n], cf_("half")[:, 0:n], ALU.pow).then_inc(rstd_ready, 1)

            def inv_std2(e):
                pool.wait_ge(var2_ready, e + 1)
                pool.tensor_tensor(rstd2[:, :], veps2[:, :], cf_("half")[:, 0:2], ALU.pow).then_inc(rstd2_ready, 1)

            def gate_wout(b):
                if after(b, 1):
                    pool.wait_ge(y_done, b)
                pool.tensor_tensor(wout_g[:, :], wout_sb[:, :], mod(b, 0), ALU.mult).then_inc(woutg_ready, 1)

            def spread_k(b, quad):
                pool.wait_ge(qk_copied, b + 1)
                if after(b, 1):
                    pool.wait_ge(scores_done, b * 8 - 3 + quad)
                pool.tensor_tensor(k_diag[:, quad, :, W:WIN], k_sb[:, :].unsqueeze(1).to_broadcast([P, 4, S]),
                                   headmask.rearrange("p (j q) -> p q j", q=4)[:, quad, :].unsqueeze(2)
                                   .to_broadcast([P, 4, S]), ALU.mult).then_inc(kdiag_pool, 1)

            def scatter(par):
                pool.reg_add(batches, batches, 1)
                pool.wait_ge(ld_x0, 32)
                pool.wait_ge(rows_ready, batches)
                pool.wait_ge(pay_ready, batches)
                for p in range(2):
                    for k in range(TOPK):
                        at = bass.IndirectOffsetOnAxis(ap=row_u[par][:, 2 * p + k:2 * p + k + 1], axis=0)
                        pool.indirect_dma_start(routed[:, :], at, pay[par][:, p, k, :], None).then_inc(scattered[par], 16)

            def batch(b, par, half, first, last):
                if not first:
                    inv_std2(b - 1)
                gate_wout(b)
                if not last:
                    for quad in (1, 2, 3):
                        spread_k(b + 1, quad)
                if first:
                    inv_std(3, 4, NT - 4)
                else:
                    scatter(1 - par)

            pool.wait_ge(ld_x0, 32)
            for p in range(2):
                pool.dma_start(routed[E * REGION + p * W:E * REGION + (p + 1) * W, :],
                               cf_("padrow", W)).then_inc(scattered[p], 16)
            inv_std(1, 0, 2)
            for quad in (1, 2, 3):
                spread_k(0, quad)
            inv_std(2, 2, 2)
            pool.wait_ge(ld_w, 64)
            pool.wait_ge(mod_in, 16)
            over_batches(pool, batch)
            inv_std2(B - 1)
            scatter(1)

            def store(s, q):
                pool.reg_add(slots, slots, 1)
                pool.wait_ge(ld_x0, 32)
                pool.wait_ge(ye_copied, slots)
                pool.wait_ge(ix_ready, slots)
                pool.indirect_dma_start(ranked[:, :], bass.IndirectOffsetOnAxis(ap=ix_u[q][:, 0:1], axis=0),
                                        y_sb[q][:, :], None, bounds_check=TOPK * TOKENS - 1,
                                        oob_is_err=False).then_inc(y_out[q], 16)

            with pool.Fori(0, N_SLOTS // 4) as k:
                for q in range(4):
                    store(k * 4 + q, q)


def constants():
    import numpy as np

    f = np.zeros((P, N_CF), np.float32)
    put = lambda name, a: f.__setitem__((slice(None), slice(*CF[name])), np.broadcast_to(a, (P, CF[name][1] - CF[name][0])))
    row = np.arange(P)[:, None]
    put("ident", np.eye(P))
    put("headmask", row // HD == np.arange(H))
    put("iota8", np.arange(E))
    put("base8", np.arange(E) * REGION)
    put("tokid", np.arange(2 * NT) // 2 * P + row + TOKENS * (np.arange(2 * NT) % 2))
    put("steps", np.tile(np.arange(NT) * P, E))
    put("tri8", (np.arange(E) <= np.arange(E)[:, None]).ravel())
    put("slot", np.repeat(np.arange(N_SLOTS), E))
    put("padrow", np.where(np.arange(PAY) == D, OUT_OF_RANGE, 0.0))
    put("half", -0.5)
    g = np.zeros((P, N_CB), np.float32)
    put = lambda name, a: g.__setitem__((slice(None), slice(*CB[name])), np.reshape(a, (P, -1)))
    put("ident", np.eye(P))
    put("before", row < np.arange(P))
    put("region", np.tile(np.arange(E) * (REGION // P), (P, 1)))
    put("ones", np.ones((P, P)))
    late = np.where(np.arange(W) > row % W, MASKED, 0.0)
    m0 = np.zeros((P, 4, 2 * W))
    m0[:W, :, :W] = MASKED
    m0[:, :, W:] = late[:, None]
    put("mask0", m0)
    put("mask1", np.repeat(late[:, None], 4, 1))
    return f, g.astype(mybir.dt.np(BF16))


def kernel(L0_attn_x, L0_attn_w_qkv, L0_attn_w_out, L0_ffn_Wg, L0_ffn_W1, L0_ffn_W3, L0_ffn_W2, L0_c, L0_wmod):
    import numpy as np
    import concourse.bacc as bacc
    from concourse.bass_utils import run_bass_kernel_spmd

    f, g = constants()
    a = lambda v: np.ascontiguousarray(v)
    w1, w3, w2 = (np.asarray(v) for v in (L0_ffn_W1, L0_ffn_W3, L0_ffn_W2))
    w2t = np.zeros((E, HIDP, D), np.float32)
    w2t[:, :HID] = w2.transpose(0, 2, 1)
    w2t = w2t.reshape(E, KT, P, D).transpose(2, 0, 1, 3).reshape(P, E, KT * D)
    we = np.concatenate([w1.transpose(2, 0, 1), w3.transpose(2, 0, 1), w2t], axis=2).reshape(P, E * WE)
    arrays = {
        "x": a(L0_attn_x), "c_t": a(np.asarray(L0_c).T), "wqkv": a(L0_attn_w_qkv), "wout": a(L0_attn_w_out),
        "wmod": a(L0_wmod), "wg_t": a(np.asarray(L0_ffn_Wg).T), "we": a(we), "cf": f, "cb": g,
    }
    nc = bacc.Bacc("TRN2", target_bir_lowering=False, num_devices=1)
    args = {k: nc.dram_tensor(k, v.shape, mybir.dt.from_np(v.dtype), kind="ExternalInput").ap()
            for k, v in arrays.items()}
    out = nc.dram_tensor("out", [B, S, D], F32, kind="ExternalOutput").ap()
    build(nc, out=out, **args)
    r = run_bass_kernel_spmd(nc, [arrays], core_ids=[0])
    return r.results[0]["out"]
```

```python
from contextlib import ExitStack

import concourse.bass as bass
from concourse import mybir

F32 = mybir.dt.float32
BF16 = mybir.dt.bfloat16
I32 = mybir.dt.int32
U32 = mybir.dt.uint32
ALU = mybir.AluOpType
ACT = mybir.ActivationFunctionType
AX_X = mybir.AxisListType.X

P = 128
B, S, D = 8, 256, 128
H, W = 16, 64
HD = D // H
E, TOPK, HID = 8, 2, 352
EPS = 1e-5
NT = B * S // P
TOKENS = B * S
REGION = TOKENS + P
N_ROWS = E * REGION + P
N_SLOTS = -(-(TOPK * TOKENS // P + E - 1) // 4) * 4
N_EARLY = ((B - 2) * TOPK * S - E * (P - 1)) // P
N_LATE = N_SLOTS - N_EARLY
PARTS = B
PART = NT // PARTS
POOL_PARTS = (0, 2, 4, 6)
PAY = D + 1
HIDP = 384
KT = HIDP // P
WE = 2 * HID + KT * D
LANE = 40
WIN = W + S
OUT_OF_RANGE = 1.0e6
MASKED = -1.0e30

CF = {}
CR = {}
CB = {}


def _columns(table, names):
    at = 0
    for name, n in names:
        table[name] = (at, at + n)
        at += n
    return at


N_CF = _columns(CF, [("ident", P), ("headmask", H), ("iota8", E), ("base8", E), ("tokid", 2 * NT),
                     ("padrow", PAY), ("half", NT)])
N_CR = _columns(CR, [("steps", E * NT), ("tri8", E * E), ("slot", N_LATE * E), ("region", E), ("fours", N_LATE // 4)])
N_CB = _columns(CB, [("ident", P), ("before", P), ("ones", P), ("region", E), ("late", 4 * W), ("none", 4 * W)])


def build(nc, x, c_t, wqkv, wout, wmod, wg_t, we, cf, cr, cb, out):
    routed = nc.dram_tensor("routed", [N_ROWS, PAY], F32, kind="Internal").ap()
    ranked = nc.dram_tensor("ranked", [TOPK * TOKENS, D], F32, kind="Internal").ap()
    mod_rows = nc.dram_tensor("mod_rows", [B, 4 * D], F32, kind="Internal").ap()

    with ExitStack() as ctx:
        def sb(name, shape, dt=F32):
            return ctx.enter_context(nc.sbuf_tensor(name, shape, dt))

        def sem(name):
            return ctx.enter_context(nc.semaphore(name))

        bank = [ctx.enter_context(nc.psum_tensor(f"bank{i}", [P, 512], F32)) for i in range(8)]
        PT_BANK = bank[3]
        O_BANK = bank[4]
        M = bank[5:8]
        XT_BANK, H1_BANK, H3_BANK = bank[0], bank[1:3], bank[3:5]
        GT_BANK, Y_BANK = (bank[5], bank[7]), bank[6]

        cf_sb = sb("cf_sb", [P, N_CF])
        cr_sb = sb("cr_sb", [1, N_CR])
        cb_sb = sb("cb_sb", [P, N_CB], BF16)
        ct_sb = sb("ct_sb", [P, B])
        wqkv_sb = sb("wqkv_sb", [P, 3 * D])
        wout_sb = sb("wout_sb", [P, D])
        wmod_sb = sb("wmod_sb", [P, 6 * D])
        wg_sb = sb("wg_sb", [P, E])
        we_sb = sb("we_sb", [P, E * WE])
        silu_c = sb("silu_c", [P, B])
        warm = sb("warm", [P, 1])
        idle = sb("idle", [P, 512], BF16)
        mod_t = sb("mod_t", [P, 2 * B])
        mod_s = sb("mod_s", [B, 4 * D])
        mod_a = sb("mod_a", [B, 2, D])
        mod_b = sb("mod_b", [B, 2, D])
        mod_bc = sb("mod_bc", [P, B * 4 * D])
        x_all = sb("x_all", [P, NT, D])
        stats = sb("stats", [P, NT, 6])
        mv = sb("mv", [P, NT * 2])
        veps = sb("veps", [P, NT])
        rstd = sb("rstd", [P, NT])
        normed = sb("normed", [P, 2, D])
        h_t = sb("h_t", [P, WIN])
        q_t = [sb(f"q_t{i}", [P, S]) for i in range(2)]
        k_sb = sb("k_sb", [P, S])
        k_diag = sb("k_diag", [P, 4, 4, WIN])
        v_lane = [sb(f"v_lane{i}", [P, 4 * H * LANE + LANE]) for i in range(2)]
        negmax = sb("negmax", [P, 4, 4])
        probs = [sb(f"probs{i}", [P, 4, P]) for i in range(2)]
        probs_t = [sb(f"probs_t{i}", [P, 4, P]) for i in range(2)]
        den = [sb(f"den{i}", [P, 2 * H]) for i in range(2)]
        rden = sb("rden", [P, 2 * H])
        rden_w = sb("rden_w", [P, 2 * H, HD])
        o_sb = sb("o_sb", [P, 2, P])
        o_n = sb("o_n", [P, 2, P])
        wout_g = sb("wout_g", [P, D])
        stats2 = sb("stats2", [P, 2, 6])
        mv2 = sb("mv2", [P, 2, 2])
        veps2 = sb("veps2", [P, 2])
        rstd2 = sb("rstd2", [P, 2])
        centred = sb("centred", [P, 2, D])
        pay = [sb(f"pay{i}", [P, 2, TOPK, PAY]) for i in range(2)]
        h2_t = sb("h2_t", [P, 2, P])
        sc8 = sb("sc8", [P, 2, E])
        top8 = sb("top8", [P, 2, 8])
        ix8 = sb("ix8", [P, 2, 8], U32)
        top_v = sb("top_v", [P, NT, TOPK])
        hot = sb("hot", [P, 2, TOPK, E])
        hot_b = sb("hot_b", [P, 2, E], BF16)
        hot_2 = sb("hot_2", [P, E], BF16)
        hot_sum = sb("hot_sum", [P, E], BF16)
        junk = sb("junk", [P, 2, TOPK, E])
        row_u = [sb(f"row_u{i}", [P, 2 * TOPK], U32) for i in range(2)]
        ends = sb("ends", [1, E])
        n_e = sb("n_e", [1, E])
        cmp_e = sb("cmp_e", [1, E, NT])
        tiles_e = sb("tiles_e", [1, E])
        cum_m = sb("cum_m", [1, E, E])
        cum_e = sb("cum_e", [1, E])
        taken = sb("taken", [1, 1 + E])
        used = sb("used", [1, E + 1])
        jump = sb("jump", [1, E])
        hop = sb("hop", [1, E])
        ge = sb("ge", [1, N_LATE, E])
        ge_t = sb("ge_t", [1, N_LATE, E])
        slot_e = sb("slot_e", [1, N_LATE])
        slot_t = sb("slot_t", [1, N_LATE])
        fours = sb("fours", [1, 1])
        begun = sb("begun", [1, N_LATE // 4])
        table = sb("table", [1, 2 * N_SLOTS + E + 1], I32)
        xt_in = [sb(f"xt_in{i}", [P, PAY]) for i in range(4)]
        ix_u = [sb(f"ix_u{i}", [P, 1], U32) for i in range(4)]
        x_t = [sb(f"x_t{i}", [P, P]) for i in range(2)]
        act1 = [sb(f"act1_{i}", [P, HID]) for i in range(2)]
        gated = [sb(f"gated{i}", [P, HIDP]) for i in range(2)]
        gated_t = [sb(f"gated_t{i}", [P, HIDP]) for i in range(2)]
        y_sb = [sb(f"y_sb{i}", [P, D]) for i in range(4)]
        fin_y = sb("fin_y", [P, NT, TOPK, D])
        fin_b = sb("fin_b", [P, NT, D])
        ex = sb("ex", [P, NT])
        exd = sb("exd", [P, NT])
        w_hi = sb("w_hi", [P, NT])
        w_lo = sb("w_lo", [P, NT])

        def cf_(name, rows=P):
            a, z = CF[name]
            return cf_sb[0:rows, a:z]

        def cr_(name):
            a, z = CR[name]
            return cr_sb[:, a:z]

        def cb_(name):
            a, z = CB[name]
            return cb_sb[:, a:z]

        ident, ident_b, headmask = cf_("ident"), cb_("ident"), cf_("headmask")

        def mod(b, which):
            return mod_bc[:, bass.ds((b * 4 + which) * D, D)]

        def x_tile(t):
            return x_all[:, bass.ds(t, 1), :].rearrange("p a d -> p (a d)")

        ld_c = sem("ld_c")
        ld_x0 = sem("ld_x0")
        ld_w = sem("ld_w")
        ld_m = sem("ld_m")
        ld_b = sem("ld_b")
        ld_o = sem("ld_o")
        ld_x = sem("ld_x")
        ld_e = sem("ld_e")
        mod_out = sem("mod_out")
        mod_in = sem("mod_in")
        silu_done = sem("silu_done")
        idle_ready = sem("idle_ready")
        mod_t_mm = sem("mod_t_mm")
        mod_t_ready = sem("mod_t_ready")
        mod_mm = sem("mod_mm")
        mod_done = sem("mod_done")
        zeroed = sem("zeroed")
        scores_done = sem("scores_done")
        negmax_done = sem("negmax_done")
        probs_done = sem("probs_done")
        pt_done = sem("pt_done")
        pt_copied = sem("pt_copied")
        pv_done = sem("pv_done")
        var_ready = sem("var_ready")
        rstd_ready = sem("rstd_ready")
        normed_ready = sem("normed_ready")
        nt_done = sem("nt_done")
        ht_ready = sem("ht_ready")
        qk_done = sem("qk_done")
        qk_copied = sem("qk_copied")
        kdiag_act = sem("kdiag_act")
        kdiag_pool = sem("kdiag_pool")
        kdiag_dve = sem("kdiag_dve")
        v_done = sem("v_done")
        v_copied = sem("v_copied")
        o_copied = sem("o_copied")
        sums_inverted = sem("sums_inverted")
        rden_ready = sem("rden_ready")
        rt_done = sem("rt_done")
        on_ready = sem("on_ready")
        woutg_ready = sem("woutg_ready")
        y_done = sem("y_done")
        x2_ready = sem("x2_ready")
        stats2_ready = sem("stats2_ready")
        mv2_ready = sem("mv2_ready")
        var2_ready = sem("var2_ready")
        rstd2_ready = sem("rstd2_ready")
        centred_ready = sem("centred_ready")
        h2_ready = sem("h2_ready")
        pay_ready = sem("pay_ready")
        h2t_done = sem("h2t_done")
        h2t_copied = sem("h2t_copied")
        gate_done = sem("gate_done")
        sc8_ready = sem("sc8_ready")
        top8_ready = sem("top8_ready")
        ix8_ready = sem("ix8_ready")
        hot1_ready = sem("hot1_ready")
        hot_ready = sem("hot_ready")
        hot2_ready = sem("hot2_ready")
        prefix_done = sem("prefix_done")
        junk_ready = sem("junk_ready")
        rows_ready = sem("rows_ready")
        scattered = [sem(f"scattered{i}") for i in range(2)]
        dve_link = sem("dve_link")
        count_done = sem("count_done")
        count_read = sem("count_read")
        table_ready = sem("table_ready")
        fours_counted = sem("fours_counted")
        fours_ready = sem("fours_ready")
        padded = [sem(f"padded{i}") for i in range(3)]
        xt_loaded = [sem(f"xt_loaded{i}") for i in range(4)]
        xt_done = sem("xt_done")
        xt_copied = sem("xt_copied")
        ix_ready = sem("ix_ready")
        h1_done = sem("h1_done")
        h3_done = sem("h3_done")
        act1_ready = sem("act1_ready")
        gated_ready = sem("gated_ready")
        gt_done = sem("gt_done")
        gt_copied = sem("gt_copied")
        ye_done = sem("ye_done")
        ye_copied = sem("ye_copied")
        y_out = [sem(f"y_out{i}") for i in range(4)]
        fin_in = [sem(f"fin_in{i}") for i in range(PARTS)]
        ex_ready = sem("ex_ready")
        w_ready = sem("w_ready")
        weighted = sem("weighted")
        summed = sem("summed")
        gated_part = [sem(f"gated_part{i}") for i in range(PARTS)]
        part_done = [sem(f"part_done{i}") for i in range(PARTS)]
        fin_out = sem("fin_out")

        SCORES_IN = [bank[q] for q in (7, 0, 1, 2, 0, 6, 1, 2)]
        SCORE_AGO = (None, 5, 4, 4, 3, None, 4, 4)

        block = ctx.enter_context(nc.Block())

        def over_batches(eng, body):
            body(0, 0, 0, True, False)
            with eng.Fori(0, B // 2 - 1) as k:
                body(k * 2 + 1, 1, k, False, False)
                body(k * 2 + 2, 0, k + 1, False, False)
            body(B - 1, 1, B // 2 - 1, False, True)

        def counter(eng, name):
            r = eng.alloc_register(f"{name}_count")
            eng.reg_mov(r, 0)
            return r

        def finish_part(eng, i):
            part = slice(PART * i, PART * i + PART)
            gb = mod(i, 3).unsqueeze(1).to_broadcast([P, PART, D])
            eng.tensor_tensor(fin_b[:, part, :], fin_b[:, part, :], gb, ALU.mult).then_inc(gated_part[i], 1)
            eng.wait_ge(gated_part[i], 1)
            eng.tensor_tensor(fin_b[:, part, :], fin_b[:, part, :], x_all[:, part, :], ALU.add).then_inc(part_done[i], 1)

        def late_fours(eng):
            eng.wait_ge(fours_ready, 1)
            return eng.value_load(table[0:1, 2 * N_SLOTS + E:2 * N_SLOTS + E + 1],
                                  min_val=(TOPK * TOKENS // P - N_EARLY) // 4, max_val=N_LATE // 4)

        WARM = (8, 5)

        def pad(eng, e, done):
            row = eng.value_load(table[0:1, 2 * N_SLOTS + e:2 * N_SLOTS + e + 1], min_val=0, max_val=N_ROWS - P)
            eng.dma_start(routed[bass.ds(row, P), :], cf_("padrow")).then_inc(done, 16)

        STAGES = (("x", 2), ("h", 1), ("t", 0), ("y", -1))

        STRAIGHT = N_EARLY - 3

        def over_slots(eng, step, aside=None):
            aside = aside or (lambda i, at: None)
            for s in range(-2, STRAIGHT):
                if s == STRAIGHT - 1:
                    n = late_fours(eng)
                step(s, s % 4, [c for c, d in STAGES if s + d >= 0], lambda at: aside(s + 2, at))
            with eng.Fori(0, n) as k:
                for r in range(4):
                    step(k * 4 + (STRAIGHT + r), (STRAIGHT + r) % 4, [c for c, _ in STAGES], lambda at: None)
            for r in range(4):
                step(n * 4 + (STRAIGHT + r), (STRAIGHT + r) % 4, [c for c, d in STAGES if d < 3 - r], lambda at: None)

        def after(s, n):
            return not isinstance(s, int) or s >= n

        @block.sync
        def _(sp):
            xv = x.rearrange("b (a p) d -> p (b a) d", p=P)
            sp.dma_start(x_all[:, 0:2, :], xv[:, 0:2, :]).then_inc(ld_x0, 16)
            sp.dma_start(ct_sb[:, :], c_t).then_inc(ld_c, 16)
            sp.dma_start(wmod_sb[:, 0:2 * D], wmod[:, 0:2 * D]).then_inc(ld_c, 16)
            sp.dma_start(cf_sb[:, :], cf).then_inc(ld_x0, 16)
            sp.dma_start(wqkv_sb[:, :], wqkv).then_inc(ld_w, 16)
            sp.dma_start(wmod_sb[:, 2 * D:6 * D], wmod[:, 2 * D:6 * D]).then_inc(ld_m, 16)
            sp.dma_start(cb_sb[:, :], cb).then_inc(ld_b, 16)
            sp.dma_start(x_all[:, 2:NT, :], xv[:, 2:NT, :]).then_inc(ld_x, 16)
            sp.dma_start(wout_sb[:, :], wout).then_inc(ld_o, 16)
            sp.dma_start(wg_sb[:, :], wg_t).then_inc(ld_o, 16)
            sp.dma_start(cr_sb[:, :], cr).then_inc(ld_o, 16)
            sp.wait_ge(mod_done, 1)
            sp.dma_start(mod_rows, mod_s[:, :]).then_inc(mod_out, 16)
            sp.wait_ge(mod_out, 16)
            sp.dma_start(mod_bc[:, :], mod_rows.rearrange("b n -> (b n)").partition_broadcast(P)).then_inc(mod_in, 16)
            sp.dma_start(we_sb[:, :], we).then_inc(ld_e, 16)

            def load(s, r):
                if after(s, 4):
                    sp.wait_ge(xt_done, s - 3)
                    sp.wait_ge(ix_ready, s - 3)
                row = sp.value_load(table[0:1, bass.ds(s, 1)], min_val=0, max_val=N_ROWS - P)
                sp.dma_start(xt_in[r][:, :], routed[bass.ds(row, P), :]).then_inc(xt_loaded[r], 16)

            sp.wait_ge(table_ready, 1)
            for r in scattered:
                sp.wait_ge(r, 16 + 64 * (B // 2 - 1))
            for s in range(N_EARLY):
                if s == N_EARLY - 2:
                    sp.wait_ge(table_ready, 2)
                    for e in range(3):
                        pad(sp, e, padded[0])
                load(s, s % 4)
            for i, n in enumerate((3, 1, 4)):
                sp.wait_ge(padded[i], 16 * n)
            for r in scattered:
                sp.wait_ge(r, 16 + 64 * (B // 2))
            n_fours = late_fours(sp)
            with sp.Fori(N_EARLY // 4, n_fours + N_EARLY // 4) as k:
                for r in range(4):
                    load(k * 4 + r, r)

            for r in range(4):
                sp.wait_ge(y_out[r], n_fours * 16 + 4 * N_EARLY)
            rv = ranked.rearrange("(t p k) d -> p t (k d)", k=TOPK, p=P)
            for i in range(PARTS):
                part = slice(PART * i, PART * (i + 1))
                sp.dma_start(fin_y[:, part, :, :].rearrange("p t k d -> p t (k d)"),
                             rv[:, part, :]).then_inc(fin_in[i], 16)
            ov = out.rearrange("b (a p) d -> p (b a) d", p=P)
            for i in range(PARTS):
                part = slice(PART * i, PART * (i + 1))
                sp.wait_ge(part_done[i], 1)
                sp.dma_start(ov[:, part, :], fin_b[:, part, :]).then_inc(fin_out, 16)
            sp.wait_ge(fin_out, 16 * PARTS)

        @block.tensor
        def _(pe):
            mm = pe.matmul
            def warm_up(n):
                for _ in range(n):
                    mm(bank[2][:, :], idle[:, 0:P], idle[:, :], start=True, stop=True)

            pe.wait_ge(idle_ready, 1)
            warm_up(WARM[0])
            pe.wait_ge(ld_c, 32)
            pe.wait_ge(silu_done, 1)
            mm(M[1][:, 0:B], wmod_sb[:, D:2 * D], silu_c[:, :], start=True, stop=True)
            mm(M[1][:, B:2 * B], wmod_sb[:, 0:D], silu_c[:, :], start=True, stop=True).then_inc(mod_t_mm, 1)

            def norm_t(b):
                pe.wait_ge(normed_ready, b + 1)
                pe.transpose(M[2][:, 0:P], normed[:, 0, :], ident)
                pe.transpose(M[2][:, P:2 * P], normed[:, 1, :], ident).then_inc(nt_done, 1)

            def project_qk(b):
                pe.wait_ge(ht_ready, b + 1)
                mm(M[2][:, 0:S], wqkv_sb[:, 0:D], h_t[:, W:WIN], start=True, stop=True)
                mm(M[2][:, S:2 * S], wqkv_sb[:, D:2 * D], h_t[:, W:WIN], start=True, stop=True).then_inc(qk_done, 1)

            def project_v():
                for c in range(4):
                    last = mm(M[0][:, c * P:(c + 1) * P], h_t[:, c * W:c * W + 2 * W], wqkv_sb[:, 2 * D:3 * D],
                              start=True, stop=True)
                last.then_inc(v_done, 1)

            def scores(b, par, i):
                g = b * 8 + i
                pair, quad = i // 4, i % 4
                if i == 0:
                    pe.wait_ge(qk_copied, b + 1)
                    pe.wait_ge(kdiag_act, b + 1)
                if 0 < i < 4 and (after(b, 1) or i == 1):
                    pe.wait_ge(kdiag_pool, b * 3 - 2 + quad if after(b, 1) else 1)
                elif i in (2, 3):
                    pe.wait_ge(kdiag_dve, i - 1)
                if i == 5:
                    if after(b, 1):
                        pe.wait_ge(x2_ready, b)
                elif i > 0 and after(g, SCORE_AGO[i]):
                    pe.wait_ge(probs_done, g + 1 - SCORE_AGO[i])
                s_bank = SCORES_IN[i]
                sv = s_bank[:, :].rearrange("p (h k) -> p h k", h=4)
                mm(sv[:, :, W:2 * W], ident_b, cb_("late").rearrange("p (h k) -> p h k", h=4),
                   start=True, stop=False, skip_group_check=True)
                if pair == 0:
                    mm(sv[0:W, :, 0:W], ident_b[:, 0:W], cb_("none").rearrange("p (h k) -> p h k", h=4),
                       start=False, stop=False, skip_group_check=True)
                for a in range(2):
                    c = 2 * pair + a
                    last = mm(sv[a * W:(a + 1) * W, :, :], q_t[par][:, c * W:(c + 1) * W],
                              k_diag[:, quad, :, c * W:c * W + 2 * W], start=False, stop=True,
                              skip_group_check=True)
                last.then_inc(scores_done, 1)

            def probs_transpose(g, i):
                pe.wait_ge(probs_done, g + 1)
                if after(g, 1):
                    pe.wait_ge(pt_copied, g)
                for j in range(4):
                    last = pe.transpose(PT_BANK[:, j * P:(j + 1) * P], probs[i % 2][:, j, :], ident)
                last.then_inc(pt_done, 1)

            def pv(b, par, i):
                pair, quad = i // 4, i % 4
                pe.wait_ge(pt_copied, b * 8 + i + 1)
                if i == 0:
                    pe.wait_ge(v_copied, b + 1)
                if quad == 0 and after(b * 8 + i, 1):
                    pe.wait_ge(o_copied, b * 2 + pair)
                for a in range(2):
                    c = 2 * pair + a
                    for j in range(4):
                        at = (c * H + 4 * j + quad) * LANE + 3 * HD - quad * HD
                        last = mm(O_BANK[32 * j:32 * j + 32, a * W:(a + 1) * W], v_lane[par][:, at:at + 32],
                                  probs_t[i % 2][:, j, a * W:(a + 1) * W], start=(quad == 0 and a == 0),
                                  stop=(quad == 3), skip_group_check=True)
                last.then_inc(pv_done, 1)

            def rden_t(e, m):
                pe.wait_ge(rden_ready, e + 1)
                for p in range(2):
                    last = pe.transpose(m[:, p * P:(p + 1) * P],
                                        rden_w[:, p * H:(p + 1) * H, :].rearrange("p h d -> p (h d)"), ident)
                last.then_inc(rt_done, 1)

            def out_project(e, m):
                pe.wait_ge(on_ready, e + 1)
                pe.wait_ge(woutg_ready, e + 1)
                for p in range(2):
                    last = mm(m[:, p * D:(p + 1) * D], o_n[:, p, :], wout_g[:, :], start=True, stop=True)
                last.then_inc(y_done, 1)

            def h2_transpose(e, par, m):
                pe.wait_ge(h2_ready, e + 1)
                for p in range(2):
                    last = pe.transpose(m[:, p * P:(p + 1) * P], pay[par][:, p, 0, 0:D], ident)
                last.then_inc(h2t_done, 1)

            def gate(e, m):
                pe.wait_ge(h2t_copied, e + 1)
                for p in range(2):
                    last = mm(m[:, p * E:(p + 1) * E], h2_t[:, p, :], wg_sb[:, :], start=True, stop=True,
                              skip_group_check=True)
                last.then_inc(gate_done, 1)

            def prefix(e, m):
                pe.wait_ge(hot_ready, e + 1)
                for p in range(2):
                    at = m[:, p * E:(p + 1) * E]
                    mm(at, cb_("before"), hot_b[:, p, :], start=True, stop=False, skip_group_check=True)
                    if p:
                        mm(at, cb_("ones"), hot_b[:, 0, :], start=False, stop=False, skip_group_check=True)
                    last = mm(at, cb_("ones"), hot_sum[:, :], start=False, stop=True, skip_group_check=True)
                last.then_inc(prefix_done, 1)

            def finish(e, par, i, areas):
                if i == 0:
                    rden_t(e, areas[0])
                if i == 1:
                    out_project(e, areas[1])
                if i == 4:
                    h2_transpose(e, par, areas[0])
                if i == 5:
                    gate(e, areas[1])
                if i == 7:
                    prefix(e, areas[1])

            def spare(b, par, i, first, last):
                if i == 0:
                    if not first:
                        pe.wait_ge(v_copied, b + 1)
                    if last:
                        pe.wait_ge(rows_ready, B - 2)
                        mm(M[2][:, 0:E], cb_("ones"), hot_sum[:, :], start=True, stop=True).then_inc(count_done, 1)
                if not first:
                    finish(b - 1, 1 - par, i, M)
                if i == 1 and not last:
                    norm_t(b + 1)
                if i == 3 and not last:
                    project_qk(b + 1)
                if i == 5 and not last:
                    if first:
                        pe.wait_ge(v_copied, 1)
                    project_v()

            def batch(b, par, half, first, last):
                for i in range(8):
                    if i + 2 < 8:
                        scores(b, par, i + 2)
                    elif not last:
                        scores(b + 1, 1 - par, i + 2 - 8)
                    probs_transpose(b * 8 + i, i)
                    if i > 0:
                        pv(b, par, i - 1)
                    elif not first:
                        pv(b - 1, 1 - par, 7)
                    spare(b, par, i, first, last)

            warm_up(WARM[1])
            pe.wait_ge(ld_x0, 32)
            norm_t(0)
            pe.wait_ge(ld_m, 16)
            mm(PT_BANK[0:B, :], silu_c[:, :], wmod_sb[:, 2 * D:6 * D], start=True, stop=True).then_inc(mod_mm, 1)
            pe.wait_ge(ld_w, 16)
            project_qk(0)
            project_v()
            pe.wait_ge(ld_b, 16)
            scores(0, 0, 0)
            scores(0, 0, 1)
            pe.wait_ge(mod_done, 1)
            pe.wait_ge(ld_o, 48)
            over_batches(pe, batch)
            pv(B - 1, 1, 7)

            pe.wait_ge(ld_e, 16)
            pe.wait_ge(table_ready, 1)
            w_at = [pe.alloc_register(f"w_at{q}") for q in range(4)]

            def weights(q, at, n):
                w = pe.snap(w_at[q], min_val=0, max_val=(E - 1) * WE)
                return we_sb[:, bass.ds(w + at, n)]

            def step(s, r, stages, aside):
                if "h" in stages:
                    n = (r + 1) % 2
                    pe.wait_ge(xt_copied, s + 2)
                    mm(H1_BANK[n][:, 0:HID], x_t[n][:, :], weights((r + 1) % 4, 0, HID), start=True,
                       stop=True).then_inc(h1_done, 1)
                    mm(H3_BANK[n][:, 0:HID], x_t[n][:, :], weights((r + 1) % 4, HID, HID), start=True,
                       stop=True).then_inc(h3_done, 1)
                if "x" in stages:
                    q = (r + 2) % 4
                    pe.reg_load(w_at[q], table[0:1, bass.ds(s + (2 + N_SLOTS), 1)])
                    pe.wait_ge(xt_loaded[q], (s + 2 - q) * 4 + 16)
                    aside("before x")
                    pe.transpose(XT_BANK[:, 0:P], xt_in[q][:, 0:D], ident).then_inc(xt_done, 1)
                if "t" in stages:
                    pe.wait_ge(gated_ready, s + 1)
                    for k in range(KT):
                        last = pe.transpose(GT_BANK[r % 2][:, k * P:(k + 1) * P],
                                            gated[r % 2][:, k * P:(k + 1) * P], ident)
                    last.then_inc(gt_done, 1)
                if "y" in stages:
                    n = (r - 1) % 2
                    pe.wait_ge(gt_copied, s)
                    if after(s, 2):
                        pe.wait_ge(ye_copied, s - 1)
                    for k in range(KT):
                        last = mm(Y_BANK[:, 0:D], gated_t[n][:, k * P:(k + 1) * P],
                                  weights((r - 1) % 4, 2 * HID + k * D, D), start=(k == 0), stop=(k == KT - 1))
                    last.then_inc(ye_done, 1)

                aside("end")

            ASIDE_READ = {0: on_ready, 1: x2_ready, 4: h2t_copied, 5: sc8_ready, 7: rows_ready}

            def aside(i, at):
                if at == "before x" and i - 1 in ASIDE_READ:
                    pe.wait_ge(ASIDE_READ[i - 1], B)
                if at == "before x" and i == 9:
                    pe.wait_ge(count_read, 2)
                if at == "end":
                    if i in ASIDE_READ or i == 8:
                        pe.wait_ge(xt_copied, i + 1)
                    finish(B - 1, 1, i, (XT_BANK, XT_BANK))
                    if i == 8:
                        mm(XT_BANK[:, 0:E], cb_("ones"), hot_sum[:, :], start=True, stop=True).then_inc(count_done, 1)

            over_slots(pe, step, aside)

        @block.scalar
        def _(act):
            act.wait_ge(ld_c, 32)
            act.activation(silu_c[:, :], ct_sb[:, :], ACT.Silu).then_inc(silu_done, 1)
            act.activation(warm[:, :], ct_sb[:, 0:1], ACT.Exp)

            def modulate(b):
                act.wait_ge(nt_done, b + 1)
                act.activation(h_t[:, W:WIN], M[2][:, 0:S], ACT.Identity, bias=mod_t[:, bass.ds(b + B, 1)],
                               scale=mod_t[:, bass.ds(b, 1)]).then_inc(ht_ready, 1)

            def copy_qk(b, par):
                act.wait_ge(qk_done, b + 1)
                act.activation(q_t[par][:, :], M[2][:, 0:S], ACT.Copy, scale=float(HD) ** -0.5)
                if after(b, 1):
                    act.wait_ge(kdiag_pool, b * 3 - 2)
                if not after(b, 2) and after(b, 1):
                    act.wait_ge(kdiag_dve, 2)
                act.copy(k_sb[:, :], M[2][:, S:2 * S]).then_inc(qk_copied, 1)

            def spread_k(b):
                if after(b, 1):
                    act.wait_ge(scores_done, b * 8 - 3)
                for j in range(4):
                    last = act.activation(k_diag[:, 0, j, W:WIN], M[2][:, S:2 * S], ACT.Copy,
                                          scale=headmask[:, 4 * j:4 * j + 1])
                last.then_inc(kdiag_act, 1)

            def copy_v(b, par):
                act.wait_ge(v_done, b + 1)
                if after(b, 2):
                    act.wait_ge(pv_done, b * 8 - 8)
                act.copy(v_lane[par][:, 0:4 * H * LANE].rearrange("p (h e) -> p h e", e=LANE)[:, :, 3 * HD:4 * HD],
                         M[0][:, :].rearrange("p (h e) -> p h e", e=HD)).then_inc(v_copied, 1)

            def softmax(b, par, i):
                g = b * 8 + i
                pair, quad = i // 4, i % 4
                act.wait_ge(negmax_done, g + 1)
                if after(g, 2):
                    act.wait_ge(pt_done, g - 1)
                for j in range(4):
                    h = pair * H + 4 * j + quad
                    last = act.activation(probs[i % 2][:, j, :], SCORES_IN[i][:, j * P:(j + 1) * P],
                                          ACT.Exp, bias=negmax[:, quad, j:j + 1], accum_out=den[par][:, h:h + 1])
                last.then_inc(probs_done, 1)

            def copy_pay(e, par):
                act.wait_ge(h2_ready, e + 1)
                act.copy(pay[par][:, :, 1, 0:D], pay[par][:, :, 0, 0:D]).then_inc(pay_ready, 1)

            def copy_h2t(e, area):
                act.wait_ge(h2t_done, e + 1)
                act.copy(h2_t[:, :, :].rearrange("p a d -> p (a d)"), area[:, 0:2 * P]).then_inc(h2t_copied, 1)

            def batch(b, par, half, first, last):
                for i in range(8):
                    softmax(b, par, i)
                    if i == 2 and not last:
                        act.wait_ge(v_done, b + 1)
                        modulate(b + 1)
                    if i == 4:
                        if not last:
                            copy_qk(b + 1, 1 - par)
                        if not first:
                            copy_pay(b - 1, 1 - par)
                    if i == 5:
                        if not first:
                            copy_h2t(b - 1, M[0])
                        if not last:
                            spread_k(b + 1)
                    if i == 6 and not last:
                        copy_v(b + 1, 1 - par)

            act.wait_ge(mod_t_ready, 1)
            act.wait_ge(zeroed, 2)
            act.wait_ge(ld_x0, 32)
            modulate(0)
            copy_qk(0, 0)
            spread_k(0)
            copy_v(0, 0)
            over_batches(act, batch)

            def step(s, r, stages, aside):
                if "h" in stages:
                    n = (r + 1) % 2
                    act.wait_ge(h1_done, s + 2)
                    if after(s, 1):
                        act.wait_ge(gated_ready, s)
                    act.activation(act1[n][:, :], H1_BANK[n][:, 0:HID], ACT.Silu).then_inc(act1_ready, 1)
                if "x" in stages:
                    act.wait_ge(xt_done, s + 3)
                    if after(s, 0):
                        act.wait_ge(h3_done, s + 1)
                    act.copy(x_t[r % 2][:, :], XT_BANK[:, 0:P]).then_inc(xt_copied, 1)
                if "y" in stages:
                    q = (r - 1) % 4
                    act.wait_ge(ye_done, s)
                    if after(s, 5):
                        act.wait_ge(y_out[q], (s - 1 - q) * 4)
                    act.copy(y_sb[q][:, :], Y_BANK[:, 0:D]).then_inc(ye_copied, 1)

                aside("a")

            def aside(i, at):
                if i == 4:
                    copy_pay(B - 1, 1)
                    copy_h2t(B - 1, XT_BANK)
                if i == 12:
                    act.wait_ge(table_ready, 2)
                    pad(act, 3, padded[1])

            over_slots(act, step, aside)
            act.wait_ge(ex_ready, 1)
            act.activation(ex[:, :], exd[:, :], ACT.Exp).then_inc(ex_ready, 1)

            act.wait_ge(w_ready, 1)
            for i in range(PARTS):
                act.wait_ge(fin_in[i], 16)
                for t in range(PART * i, PART * (i + 1)):
                    last = act.activation(fin_b[:, t, :], fin_y[:, t, 1, :], ACT.Copy, scale=w_lo[:, t:t + 1])
                last.then_inc(weighted, 1)

        @block.vector
        def _(dve):
            links = counter(dve, "links")

            def link(ins, on_its_own=False):
                ins.then_inc(dve_link, 1)
                dve.reg_add(links, links, 1)
                if on_its_own:
                    dve.wait_ge(ld_x0, 32)
                dve.wait_ge(dve_link, links)

            dve.memset(idle[:, :], 0.0).then_inc(idle_ready, 1)
            dve.memset(h_t[:, 0:W], 0.0)
            for i in range(2):
                last = dve.memset(gated[i][:, HID:HIDP], 0.0)
            last.then_inc(zeroed, 1)

            def norm_stats(t, n):
                for i in range(t, t + n):
                    last = dve.bn_stats(stats[:, i, :], x_all[:, i, :])
                link(last, on_its_own=True)
                for i in range(t, t + n):
                    last = dve.bn_aggr(mv[:, 2 * i:2 * i + 2], stats[:, i, :])
                link(last)
                return dve.tensor_scalar(veps[:, t:t + n], mv[:, :].rearrange("p (t k) -> p t k", k=2)[:, t:t + n, 1],
                                         EPS, None, ALU.add)

            def norm(b):
                for p in range(2):
                    t = b * 2 + p
                    last = dve.tensor_scalar(normed[:, p, :], x_tile(t), mv[:, bass.ds(t * 2, 1)],
                                             rstd[:, bass.ds(t, 1)], ALU.subtract, ALU.mult)
                last.then_inc(normed_ready, 1)

            dve.wait_ge(ld_x0, 32)
            norm_stats(0, 2).then_inc(var_ready, 1)
            dve.wait_ge(mod_t_mm, 1)
            dve.tensor_scalar(mod_t[:, 0:B], M[1][:, 0:B], 1.0, None, ALU.add)
            dve.tensor_copy(mod_t[:, B:2 * B], M[1][:, B:2 * B]).then_inc(mod_t_ready, 1)
            dve.wait_ge(rstd_ready, 1)
            norm(0)
            dve.wait_ge(mod_mm, 1)
            gates = PT_BANK[0:B, :].rearrange("b (k d) -> b k d", k=4)[:, 0:4:3, :]
            mod_g = mod_s[:, :].rearrange("b (k d) -> b k d", k=4)[:, 0:4:3, :]
            dve.tensor_scalar(mod_s[:, D:2 * D], PT_BANK[0:B, 2 * D:3 * D], 1.0, None, ALU.add)
            link(dve.tensor_scalar(mod_a[:, :, :], gates, -1.0, None, ALU.mult))
            dve.tensor_copy(mod_s[:, 2 * D:3 * D], PT_BANK[0:B, D:2 * D])
            link(dve.tensor_tensor(mod_b[:, :, :], mod_a[:, :, :], gates, ALU.max))
            dve.tensor_scalar(mod_b[:, :, :], mod_b[:, :, :], 0.25, None, ALU.max)
            link(dve.tensor_scalar(mod_a[:, :, :], gates, 0.0, 2.0, ALU.is_ge, ALU.mult))
            dve.scalar_tensor_tensor(out=mod_g, in0=mod_a[:, :, :], scalar=-1.0, in1=mod_b[:, :, :], op0=ALU.add,
                                     op1=ALU.mult).then_inc(mod_done, 1)

            def spread_k(quad):
                dve.wait_ge(qk_copied, 1)
                dve.tensor_tensor(k_diag[:, quad, :, W:WIN], k_sb[:, :].unsqueeze(1).to_broadcast([P, 4, S]),
                                  headmask.rearrange("p (j q) -> p q j", q=4)[:, quad, :].unsqueeze(2)
                                  .to_broadcast([P, 4, S]), ALU.mult).then_inc(kdiag_dve, 1)

            def neg_max(b, i):
                dve.wait_ge(scores_done, b * 8 + i + 1)
                dve.tensor_reduce(negmax[:, i % 4, :], SCORES_IN[i][:, :].rearrange("p (h k) -> p h k", h=4),
                                  AX_X, ALU.max, negate=True).then_inc(negmax_done, 1)

            def copy_probs_t(g, i):
                dve.wait_ge(pt_done, g + 1)
                if after(g, 2):
                    dve.wait_ge(pv_done, g - 1)
                dve.tensor_copy(probs_t[i % 2][:, :, :].rearrange("p h q -> p (h q)"), PT_BANK[:, :]).then_inc(pt_copied, 1)

            finish = counter(dve, "finish")

            def wait_alone(sem_):
                dve.wait_ge(ld_x0, 32)
                dve.wait_ge(sem_, finish)

            def copy_output(b, p):
                dve.wait_ge(pv_done, b * 8 + 4 * p + 4)
                dve.tensor_copy(o_sb[:, p, :], O_BANK[:, 0:P]).then_inc(o_copied, 1)

            def invert_sums(par):
                dve.reciprocal(rden[:, :], den[par][:, :]).then_inc(sums_inverted, 1)

            def widen_sums():
                dve.wait_ge(sums_inverted, finish)
                dve.tensor_copy(rden_w[:, :, :], rden[:, :].unsqueeze(2).to_broadcast([P, 2 * H, HD])).then_inc(rden_ready, 1)

            def divide_output(e, area):
                dve.wait_ge(rt_done, finish)
                dve.wait_ge(o_copied, e * 2 + 2)
                dve.tensor_tensor(o_n[:, :, :].rearrange("p a d -> p (a d)"), area[:, 0:2 * P],
                                  o_sb[:, :, :].rearrange("p a d -> p (a d)"), ALU.mult).then_inc(on_ready, 1)

            def add_residual(e, area):
                dve.wait_ge(y_done, finish)
                x2 = x_all[:, bass.ds(e * 2, 2), :]
                dve.tensor_tensor(x2, area[:, 0:2 * D].rearrange("p (a d) -> p a d", a=2), x2,
                                  ALU.add).then_inc(x2_ready, 1)

            def stats_2(e):
                wait_alone(x2_ready)
                for p in range(2):
                    last = dve.bn_stats(stats2[:, p, :], x_tile(e * 2 + p))
                last.then_inc(stats2_ready, 1)

            def aggregate_2():
                wait_alone(stats2_ready)
                for p in range(2):
                    last = dve.bn_aggr(mv2[:, p, :], stats2[:, p, :])
                last.then_inc(mv2_ready, 1)

            def variance_2():
                dve.wait_ge(mv2_ready, finish)
                dve.tensor_scalar(veps2[:, :], mv2[:, :, 1], EPS, None, ALU.add).then_inc(var2_ready, 1)

            def centre_2(e):
                for p in range(2):
                    last = dve.scalar_tensor_tensor(out=centred[:, p, :], in0=x_tile(e * 2 + p), scalar=mv2[:, p, 0:1],
                                                    in1=mod(e, 1), op0=ALU.subtract, op1=ALU.mult)
                last.then_inc(centred_ready, 1)

            def modulate_2(e, par, half):
                dve.wait_ge(scattered[par], half * 64 + 16)
                dve.tensor_copy(pay[par][:, :, :, D],
                                cf_("tokid")[:, bass.ds(e * 4, 4)].rearrange("p (a k) -> p a k", a=2))
                dve.wait_ge(rstd2_ready, finish)
                dve.wait_ge(centred_ready, finish)
                for p in range(2):
                    last = dve.scalar_tensor_tensor(out=pay[par][:, p, 0, 0:D], in0=centred[:, p, :],
                                                    scalar=rstd2[:, p:p + 1], in1=mod(e, 2), op0=ALU.mult,
                                                    op1=ALU.add)
                last.then_inc(h2_ready, 1)

            def copy_scores(area):
                dve.wait_ge(gate_done, finish)
                dve.tensor_copy(sc8[:, :, :].rearrange("p a e -> p (a e)"), area[:, 0:2 * E]).then_inc(sc8_ready, 1)

            def top_scores():
                wait_alone(sc8_ready)
                for p in range(2):
                    last = dve.max(top8[:, p, :], sc8[:, p, :])
                last.then_inc(top8_ready, 1)

            def top_experts(e):
                wait_alone(top8_ready)
                for p in range(2):
                    last = dve.max_index(ix8[:, p, :], top8[:, p, :], sc8[:, p, :])
                last.then_inc(ix8_ready, 1)
                dve.tensor_copy(top_v[:, bass.ds(e * 2, 2), :], top8[:, :, 0:TOPK])

            def one_hot():
                dve.wait_ge(ix8_ready, finish)
                for p in range(2):
                    last = dve.tensor_tensor(hot[:, p, :, :], ix8[:, p, 0:TOPK].unsqueeze(2).to_broadcast([P, TOPK, E]),
                                             cf_("iota8").unsqueeze(1).to_broadcast([P, TOPK, E]), ALU.is_equal)
                last.then_inc(hot1_ready, 1)

            def sum_ranks():
                dve.wait_ge(hot1_ready, finish)
                dve.tensor_tensor(hot_b[:, :, :], hot[:, :, 0, :], hot[:, :, 1, :], ALU.add).then_inc(hot_ready, 1)

            def sum_tiles():
                dve.wait_ge(hot_ready, finish)
                dve.tensor_tensor(hot_2[:, :], hot_b[:, 0, :], hot_b[:, 1, :], ALU.add).then_inc(hot2_ready, 1)

            def choose_rows(par, area):
                dve.wait_ge(prefix_done, finish)
                for p in range(2):
                    last = dve.tensor_tensor(junk[:, p, :, :], hot[:, p, :, :],
                                             area[:, p * E:(p + 1) * E].unsqueeze(1).to_broadcast([P, TOPK, E]), ALU.mult)
                last.then_inc(junk_ready, 1)
                dve.wait_ge(hot2_ready, finish)
                dve.tensor_tensor(hot_sum[:, :], hot_sum[:, :], hot_2[:, :], ALU.add)
                dve.wait_ge(junk_ready, finish)
                with nc.allow_low_precision(reason="one term of a sum is not zero, and whole"):
                    dve.tensor_reduce(row_u[par][:, :], junk[:, :, :, :].rearrange("p a k e -> p (a k) e"), AX_X,
                                      ALU.add).then_inc(rows_ready, 1)

            def finish_a(i, e, areas):
                if i == 0:
                    dve.reg_add(finish, finish, 1)
                    widen_sums()
                if i == 1:
                    divide_output(e, areas[0])
                if i == 2:
                    add_residual(e, areas[1])
                if i == 3:
                    variance_2()
                if i == 6:
                    top_scores()
                if i == 7:
                    sum_ranks()

            def finish_b(i, e):
                if i == 2:
                    stats_2(e)
                if i == 3:
                    centre_2(e)
                if i == 6:
                    top_experts(e)
                if i == 7:
                    sum_tiles()

            def finish_c(i, e, par, half, areas):
                if i == 0:
                    copy_output(e, 1)
                if i == 2:
                    aggregate_2()
                if i == 3:
                    modulate_2(e, par, half)
                if i == 5:
                    copy_scores(areas[1])
                if i == 6:
                    one_hot()
                if i == 7:
                    choose_rows(par, areas[1])

            def read_counts(area, n):
                dve.wait_ge(count_done, n)
                dve.tensor_copy(ends[:, :], area[0:1, 0:E]).then_inc(count_read, 1)

            def table_tiles(early):
                dve.wait_ge(count_read, 1 if early else 2)
                link(dve.scalar_tensor_tensor(out=n_e[:, :], in0=ends[:, :], scalar=float(P - 1) if early else 0.0,
                                              in1=cf_("base8", 1), op0=ALU.subtract, op1=ALU.subtract))
                if not early:
                    dve.tensor_copy(table[:, 2 * N_SLOTS:2 * N_SLOTS + E], ends[:, :])
                link(dve.tensor_tensor(cmp_e[:, :, :], n_e[:, :].unsqueeze(2).to_broadcast([1, E, NT]),
                                       cr_("steps").rearrange("p (e j) -> p e j", e=E), ALU.is_gt))
                link(dve.tensor_reduce(tiles_e[:, :], cmp_e[:, :, :], AX_X, ALU.add))
                if not early:
                    link(dve.tensor_tensor(tiles_e[:, :], tiles_e[:, :], used[:, 0:E], ALU.subtract))

            def table_sums(early):
                link(dve.tensor_tensor(cum_m[:, :, :], cr_("tri8").rearrange("p (e f) -> p e f", e=E),
                                       tiles_e[:, :].unsqueeze(1).to_broadcast([1, E, E]), ALU.mult))
                dve.tensor_tensor(jump[:, :], cr_("region") if early else hop[:, :], tiles_e[:, :], ALU.subtract)
                link(dve.tensor_reduce(cum_e[:, :], cum_m[:, :, :], AX_X, ALU.add))

            def table_passed(n):
                slots = cr_("slot").rearrange("p (s e) -> p s e", e=E)[:, 0:n, :]
                link(dve.tensor_tensor(ge[:, 0:n, :], slots, cum_e[:, :].unsqueeze(1).to_broadcast([1, n, E]), ALU.is_ge))
                dve.tensor_reduce(slot_e[:, 0:n], ge[:, 0:n, :], AX_X, ALU.add)
                link(dve.tensor_tensor(ge_t[:, 0:n, :], ge[:, 0:n, :], jump[:, :].unsqueeze(1).to_broadcast([1, n, E]),
                                       ALU.mult))

            def table_rows(n, first):
                link(dve.tensor_reduce(slot_t[:, 0:n], ge_t[:, 0:n, :], AX_X, ALU.add))
                dve.tensor_scalar(slot_e[:, 0:n], slot_e[:, 0:n], float(E - 1), None, ALU.min)
                slots = cr_("slot").rearrange("p (s e) -> p s e", e=E)[:, 0:n, 0]
                link(dve.scalar_tensor_tensor(out=slot_t[:, 0:n], in0=slot_t[:, 0:n], scalar=used[:, 0:1], in1=slots,
                                              op0=ALU.add, op1=ALU.add))
                dve.tensor_scalar(table[:, N_SLOTS + first:N_SLOTS + first + n], slot_e[:, 0:n], float(WE), None, ALU.mult)
                dve.tensor_scalar(table[:, first:first + n], slot_t[:, 0:n], float(E * REGION // P), float(P),
                                  ALU.min, ALU.mult).then_inc(table_ready, 1)

            def table_used():
                link(dve.tensor_scalar(taken[:, 1:], cum_e[:, :], float(N_EARLY), None, ALU.min))
                link(dve.tensor_tensor(used[:, 0:E], taken[:, 1:], taken[:, 0:E], ALU.subtract))
                link(dve.tensor_tensor(hop[:, :], used[:, 1:], used[:, 0:E], ALU.subtract))
                link(dve.tensor_tensor(hop[:, :], hop[:, :], cr_("region"), ALU.add))

            def batch(b, par, half, first, last):
                e, epar = b - 1, 1 - par
                ehalf = half if par else half - 1
                for i in range(8):
                    if not first:
                        finish_a(i, e, M)
                    copy_probs_t(b * 8 + i, i)
                    if i == 0 and not last:
                        dve.wait_ge(rstd_ready, 2 if first else 3)
                        dve.wait_ge(nt_done, b + 1)
                        norm(b + 1)
                    if not first:
                        finish_b(i, e)
                    if i == 7:
                        invert_sums(par)
                    if i + 2 < 8:
                        neg_max(b, i + 2)
                    elif not last:
                        neg_max(b + 1, i + 2 - 8)
                    if first and 1 <= i < 7:
                        done = norm_stats(2 + 2 * i, 2)
                        if i == 6:
                            done.then_inc(var_ready, 1)
                    if i == 4:
                        copy_output(b, 0)
                    if not first:
                        finish_c(i, e, epar, ehalf, M)
                    if last:
                        if i == 1:
                            read_counts(M[2], 1)
                            table_tiles(True)
                        if i == 2:
                            table_sums(True)
                        if i == 3:
                            table_passed(N_EARLY)
                        if i == 4:
                            table_rows(N_EARLY, 0)
                if first:
                    dve.wait_ge(mod_in, 16)

            spread_k(2)
            neg_max(0, 0)
            neg_max(0, 1)
            spread_k(3)
            dve.wait_ge(ld_x, 16)
            norm_stats(2, 2).then_inc(var_ready, 1)
            dve.wait_ge(ld_b, 16)
            dve.tensor_copy(hot_sum[:, :], cb_("region"))
            dve.memset(taken[:, 0:1], 0.0)
            dve.memset(used[:, :], 0.0)
            dve.wait_ge(ld_o, 48)
            over_batches(dve, batch)

            def difference():
                dve.tensor_tensor(exd[:, :], top_v[:, :, 1], top_v[:, :, 0], ALU.subtract).then_inc(ex_ready, 1)

            def rank_weights():
                dve.wait_ge(ex_ready, 2)
                link(dve.tensor_scalar(exd[:, :], ex[:, :], 1.0, None, ALU.add))
                link(dve.reciprocal(w_hi[:, :], exd[:, :]))
                dve.tensor_tensor(w_lo[:, :], ex[:, :], w_hi[:, :], ALU.mult).then_inc(w_ready, 1)

            def aside(i, at):
                areas = (XT_BANK, XT_BANK)
                if at == "a":
                    finish_a(i, B - 1, areas)
                    if i == 9:
                        read_counts(XT_BANK, 2)
                    if i == 10:
                        table_passed(N_LATE)
                if at == "b":
                    finish_b(i, B - 1)
                    if i == 9:
                        table_tiles(False)
                if at == "c":
                    finish_c(i, B - 1, 1, (B - 1) // 2, areas)
                    if i == 4:
                        table_used()
                    if i == 9:
                        table_sums(False)
                    if i == 10:
                        table_rows(N_LATE, N_EARLY)
                        link(dve.tensor_scalar(begun[:, :], cr_("fours"), cum_e[:, E - 1:E], None, ALU.is_lt))
                        dve.tensor_reduce(fours[:, :], begun[:, :], AX_X, ALU.add).then_inc(fours_counted, 1)
                    if i == 11:
                        dve.wait_ge(fours_counted, 1)
                        dve.tensor_copy(table[:, 2 * N_SLOTS + E:], fours[:, :]).then_inc(fours_ready, 1)
                        difference()

            def step(s, r, stages, aside):
                aside("a")
                if "h" in stages:
                    n = (r + 1) % 2
                    dve.wait_ge(h3_done, s + 2)
                    dve.wait_ge(act1_ready, s + 2)
                    if after(s, 1):
                        dve.wait_ge(gt_done, s)
                    dve.tensor_tensor(gated[n][:, 0:HID], H3_BANK[n][:, 0:HID], act1[n][:, :],
                                      ALU.mult).then_inc(gated_ready, 1)
                aside("b")
                if "h" in stages:
                    q = (r + 1) % 4
                    dve.wait_ge(xt_loaded[q], (s + 1 - q) * 4 + 16)
                    if after(s, 3):
                        dve.wait_ge(y_out[q], (s + 1 - q) * 4)
                    dve.tensor_copy(ix_u[q][:, :], xt_in[q][:, D:D + 1]).then_inc(ix_ready, 1)
                if "t" in stages:
                    dve.wait_ge(gt_done, s + 1)
                    if after(s, 2):
                        dve.wait_ge(ye_done, s - 1)
                    dve.tensor_copy(gated_t[r % 2][:, :], GT_BANK[r % 2][:, 0:HIDP]).then_inc(gt_copied, 1)

                aside("c")

            over_slots(dve, step, aside)
            rank_weights()

            for i in range(PARTS):
                dve.wait_ge(weighted, i + 1)
                for t in range(PART * i, PART * (i + 1)):
                    last = dve.scalar_tensor_tensor(out=fin_b[:, t, :], in0=fin_y[:, t, 0, :], scalar=w_hi[:, t:t + 1],
                                                    in1=fin_b[:, t, :], op0=ALU.mult, op1=ALU.add)
                last.then_inc(summed, 1)
                if i not in POOL_PARTS:
                    dve.wait_ge(summed, i + 1)
                    finish_part(dve, i)

        @block.gpsimd
        def _(pool):
            batches, slots = counter(pool, "batches"), counter(pool, "slots")
            for v in v_lane:
                pool.memset(v[:, :], 0.0)
            pool.memset(k_diag[:, :, :, 0:W].rearrange("p a b w -> p (a b) w"), 0.0).then_inc(zeroed, 1)

            def inv_std(count, t, n):
                pool.wait_ge(var_ready, count)
                pool.tensor_tensor(rstd[:, t:t + n], veps[:, t:t + n], cf_("half")[:, 0:n], ALU.pow).then_inc(rstd_ready, 1)

            def inv_std2(e):
                pool.wait_ge(var2_ready, e + 1)
                pool.tensor_tensor(rstd2[:, :], veps2[:, :], cf_("half")[:, 0:2], ALU.pow).then_inc(rstd2_ready, 1)

            def gate_wout(b):
                if after(b, 1):
                    pool.wait_ge(y_done, b)
                pool.tensor_tensor(wout_g[:, :], wout_sb[:, :], mod(b, 0), ALU.mult).then_inc(woutg_ready, 1)

            def spread_k(b, quad):
                pool.wait_ge(qk_copied, b + 1)
                if after(b, 1):
                    pool.wait_ge(scores_done, b * 8 - 3 + quad)
                pool.tensor_tensor(k_diag[:, quad, :, W:WIN], k_sb[:, :].unsqueeze(1).to_broadcast([P, 4, S]),
                                   headmask.rearrange("p (j q) -> p q j", q=4)[:, quad, :].unsqueeze(2)
                                   .to_broadcast([P, 4, S]), ALU.mult).then_inc(kdiag_pool, 1)

            def scatter_tile(par, p):
                for k in range(TOPK):
                    at = bass.IndirectOffsetOnAxis(ap=row_u[par][:, 2 * p + k:2 * p + k + 1], axis=0)
                    pool.indirect_dma_start(routed[:, :], at, pay[par][:, p, k, :], None).then_inc(scattered[par], 16)

            def rows_chosen():
                pool.reg_add(batches, batches, 1)
                pool.wait_ge(ld_x0, 32)
                pool.wait_ge(rows_ready, batches)
                pool.wait_ge(pay_ready, batches)

            def scatter(par):
                rows_chosen()
                for p in range(2):
                    scatter_tile(par, p)

            def batch(b, par, half, first, last):
                if not first:
                    inv_std2(b - 1)
                gate_wout(b)
                if not last:
                    for quad in (1, 2, 3):
                        spread_k(b + 1, quad)
                if first:
                    inv_std(3, 4, NT - 4)
                else:
                    scatter(1 - par)

            pool.wait_ge(ld_x0, 32)
            inv_std(1, 0, 2)
            spread_k(0, 1)
            inv_std(2, 2, 2)
            pool.wait_ge(ld_o, 48)
            for p in range(2):
                pool.dma_start(routed[E * REGION + p * W:E * REGION + (p + 1) * W, :],
                               cf_("padrow", W)).then_inc(scattered[p], 16)
            pool.wait_ge(mod_in, 16)
            over_batches(pool, batch)
            inv_std2(B - 1)

            def store(s, q):
                pool.reg_add(slots, slots, 1)
                pool.wait_ge(ld_x0, 32)
                pool.wait_ge(ye_copied, slots)
                pool.wait_ge(ix_ready, slots)
                pool.indirect_dma_start(ranked[:, :], bass.IndirectOffsetOnAxis(ap=ix_u[q][:, 0:1], axis=0),
                                        y_sb[q][:, :], None, bounds_check=TOPK * TOKENS - 1,
                                        oob_is_err=False).then_inc(y_out[q], 16)

            for s in range(4):
                store(s, s)
            rows_chosen()
            scatter_tile(1, 0)
            store(4, 0)
            scatter_tile(1, 1)
            for s in range(5, 8):
                store(s, s % 4)
            pool.wait_ge(table_ready, 2)
            for s in range(8, 12):
                for e in (2 * s - 12, 2 * s - 11):
                    if e < E:
                        pad(pool, e, padded[2])
                store(s, s % 4)
            with pool.Fori(3, late_fours(pool) + N_EARLY // 4) as k:
                for q in range(4):
                    store(k * 4 + q, q)

            for i in POOL_PARTS:
                pool.wait_ge(summed, i + 1)
                finish_part(pool, i)


def constants():
    import numpy as np

    f = np.zeros((P, N_CF), np.float32)
    put = lambda name, a: f.__setitem__((slice(None), slice(*CF[name])), np.broadcast_to(a, (P, CF[name][1] - CF[name][0])))
    row = np.arange(P)[:, None]
    put("ident", np.eye(P))
    put("headmask", row // HD == np.arange(H))
    put("iota8", np.arange(E))
    put("base8", np.arange(E) * REGION)
    put("tokid", (np.arange(2 * NT) // 2 * P + row) * TOPK + np.arange(2 * NT) % 2)
    put("padrow", np.where(np.arange(PAY) == D, OUT_OF_RANGE, 0.0))
    put("half", -0.5)
    v = np.zeros((1, N_CR), np.float32)
    put = lambda name, a: v.__setitem__((slice(None), slice(*CR[name])), a)
    put("steps", np.tile(np.arange(NT) * P, E))
    put("tri8", (np.arange(E) <= np.arange(E)[:, None]).ravel())
    put("slot", np.repeat(np.arange(N_LATE), E))
    put("fours", np.arange(N_LATE // 4) * 4)
    put("region", np.where(np.arange(E) < E - 1, REGION // P, 2 * E * REGION // P))
    g = np.zeros((P, N_CB), np.float32)
    put = lambda name, a: g.__setitem__((slice(None), slice(*CB[name])), np.reshape(a, (P, -1)))
    put("ident", np.eye(P))
    put("before", row < np.arange(P))
    put("region", np.tile(np.arange(E) * (REGION // P), (P, 1)))
    put("ones", np.ones((P, P)))
    late = np.where(np.arange(W) > row % W, MASKED, 0.0)
    put("late", np.repeat(late[:, None], 4, 1))
    put("none", np.full((P, 4 * W), MASKED))
    return f, v, g.astype(mybir.dt.np(BF16))


def kernel(L0_attn_x, L0_attn_w_qkv, L0_attn_w_out, L0_ffn_Wg, L0_ffn_W1, L0_ffn_W3, L0_ffn_W2, L0_c, L0_wmod):
    import numpy as np
    import concourse.bacc as bacc
    from concourse.bass_utils import run_bass_kernel_spmd

    f, v, g = constants()
    a = lambda w: np.ascontiguousarray(w)
    w1, w3, w2 = (np.asarray(w) for w in (L0_ffn_W1, L0_ffn_W3, L0_ffn_W2))
    w2t = np.zeros((E, HIDP, D), np.float32)
    w2t[:, :HID] = w2.transpose(0, 2, 1)
    w2t = w2t.reshape(E, KT, P, D).transpose(2, 0, 1, 3).reshape(P, E, KT * D)
    we = np.concatenate([w1.transpose(2, 0, 1), w3.transpose(2, 0, 1), w2t], axis=2).reshape(P, E * WE)
    arrays = {
        "x": a(L0_attn_x), "c_t": a(np.asarray(L0_c).T), "wqkv": a(L0_attn_w_qkv), "wout": a(L0_attn_w_out),
        "wmod": a(L0_wmod), "wg_t": a(np.asarray(L0_ffn_Wg).T), "we": a(we), "cf": f, "cr": v, "cb": g,
    }
    nc = bacc.Bacc("TRN2", target_bir_lowering=False, num_devices=1)
    args = {k: nc.dram_tensor(k, w.shape, mybir.dt.from_np(w.dtype), kind="ExternalInput").ap()
            for k, w in arrays.items()}
    out = nc.dram_tensor("out", [B, S, D], F32, kind="ExternalOutput").ap()
    build(nc, out=out, **args)
    r = run_bass_kernel_spmd(nc, [arrays], core_ids=[0])
    return r.results[0]["out"]
```
